# Optimizing a Trainium2 kernel written in Bass

```python
import numpy as np
import jax
import jax.numpy as jnp

def _softmax(x, axis=-1):
    return jax.nn.softmax(x, axis=axis)

def _gelu(x):
    return jax.nn.gelu(x, approximate=True)

def _silu(x):
    return jax.nn.silu(x)

def _sigmoid(x):
    return jax.nn.sigmoid(x)

def _layernorm(x, axis=-1, eps=1e-05):
    m = jnp.mean(x, axis=axis, keepdims=True)
    v = jnp.var(x, axis=axis, keepdims=True)
    return (x - m) / jnp.sqrt(v + eps)

def _scatter_add(tgt, idx, src, axis=0):
    return tgt.at[idx].add(src)

def _segment_sum(src, seg, n):
    return jax.ops.segment_sum(src, seg, n)
kernel_name = 'mk_seq_postln_d1_jaxref_r2_e5f0d8'

def setup_inputs(seed: int=0):
    np.random.seed(seed)
    _w = jnp.asarray

    def _L0_attn_setup():
        import jax, jax.numpy as jnp
        import numpy as np
        from jax import lax
        NUM_LEVELS = 2
        NUM_HEADS = 16
        LN_EPS = 1e-05
        ATTN_EPS = 1e-06

        def dwconv(x, filt):
            C = x.shape[-1]
            return lax.conv_general_dilated(x, filt[:, None, :], window_strides=(1,), padding='SAME', dimension_numbers=('NWC', 'WIO', 'NWC'), feature_group_count=C)

        def linear_attention(x, num_heads):
            B, N, C = x.shape
            d = C // num_heads
            h = x.reshape(B, N, num_heads, d)
            q = jax.nn.elu(h) + 1.0
            k = q
            v = h
            kv = jnp.einsum('bnhd,bnhe->bhde', k, v)
            z = k.sum(axis=1)
            num = jnp.einsum('bnhd,bhde->bnhe', q, kv)
            den = jnp.einsum('bnhd,bhd->bnh', q, z)[..., None] + ATTN_EPS
            return (num / den).reshape(B, N, C)

        def layer_norm(x, gamma, beta):
            mu = jnp.mean(x, axis=-1, keepdims=True)
            var = jnp.mean(jnp.square(x - mu), axis=-1, keepdims=True)
            return (x - mu) * lax.rsqrt(var + LN_EPS) * gamma + beta
        key = jax.random.key(seed)
        ks = jax.random.split(key, 7)
        B, S, C, K = (8, 2048, 512, 4)
        x = jax.random.normal(ks[0], (B, S, C), dtype=jnp.float32)
        scale = 1.0 / np.sqrt(K)
        h_filter = jax.random.normal(ks[1], (K, C), dtype=jnp.float32) * scale
        g_filter = jax.random.normal(ks[2], (K, C), dtype=jnp.float32) * scale
        h_synth = jax.random.normal(ks[3], (K, C), dtype=jnp.float32) * scale
        g_synth = jax.random.normal(ks[4], (K, C), dtype=jnp.float32) * scale
        norm_gamma = jnp.ones((C,), dtype=jnp.float32)
        norm_beta = jnp.zeros((C,), dtype=jnp.float32)
        return {'x': x, 'h_filter': h_filter, 'g_filter': g_filter, 'h_synth': h_synth, 'g_synth': g_synth, 'norm_gamma': norm_gamma, 'norm_beta': norm_beta}
    _L0_attn_in = _L0_attn_setup()

    def _L0_ffn_setup():
        import jax, jax.numpy as jnp
        import numpy as np
        DIM = 512
        HIDDEN = 1536
        SCALE = 1.0 / 127.0

        def _dequant(w_int, dtype):
            return w_int.astype(dtype) * jnp.asarray(SCALE, dtype)
        key = jax.random.key(seed)
        k_x, k_g, k_u, k_d = jax.random.split(key, 4)
        x = jax.random.normal(k_x, (4, 1024, DIM), dtype=jnp.float32)
        w_gate = jax.random.randint(k_g, (HIDDEN, DIM), -127, 128, dtype=jnp.int32)
        w_up = jax.random.randint(k_u, (HIDDEN, DIM), -127, 128, dtype=jnp.int32)
        w_down = jax.random.randint(k_d, (DIM, HIDDEN), -127, 128, dtype=jnp.int32)
        return {'x': x, 'w_gate': w_gate, 'w_up': w_up, 'w_down': w_down}
    _L0_ffn_in = _L0_ffn_setup()
    _d = {'L0_attn_x': _L0_attn_in['x'], 'L0_attn_h_filter': _L0_attn_in['h_filter'], 'L0_attn_g_filter': _L0_attn_in['g_filter'], 'L0_attn_h_synth': _L0_attn_in['h_synth'], 'L0_attn_g_synth': _L0_attn_in['g_synth'], 'L0_attn_norm_gamma': _L0_attn_in['norm_gamma'], 'L0_attn_norm_beta': _L0_attn_in['norm_beta'], 'L0_ffn_w_gate': _L0_ffn_in['w_gate'], 'L0_ffn_w_up': _L0_ffn_in['w_up'], 'L0_ffn_w_down': _L0_ffn_in['w_down']}
    _x0 = _d['L0_attn_x']
    _d['L0_attn_x'] = jax.random.normal(jax.random.fold_in(jax.random.key(seed), 1), (2, 4096, 512), dtype=_x0.dtype)
    del _x0
    return _d

def reference(L0_attn_x, L0_attn_h_filter, L0_attn_g_filter, L0_attn_h_synth, L0_attn_g_synth, L0_attn_norm_gamma, L0_attn_norm_beta, L0_ffn_w_gate, L0_ffn_w_up, L0_ffn_w_down):

    def _L0_attn_ref(x, h_filter, g_filter, h_synth, g_synth, norm_gamma, norm_beta):
        import jax, jax.numpy as jnp
        import numpy as np
        from jax import lax
        NUM_LEVELS = 2
        NUM_HEADS = 16
        LN_EPS = 1e-05
        ATTN_EPS = 1e-06

        def dwconv(x, filt):
            C = x.shape[-1]
            return lax.conv_general_dilated(x, filt[:, None, :], window_strides=(1,), padding='SAME', dimension_numbers=('NWC', 'WIO', 'NWC'), feature_group_count=C)

        def linear_attention(x, num_heads):
            B, N, C = x.shape
            d = C // num_heads
            h = x.reshape(B, N, num_heads, d)
            q = jax.nn.elu(h) + 1.0
            k = q
            v = h
            kv = jnp.einsum('bnhd,bnhe->bhde', k, v)
            z = k.sum(axis=1)
            num = jnp.einsum('bnhd,bhde->bnhe', q, kv)
            den = jnp.einsum('bnhd,bhd->bnh', q, z)[..., None] + ATTN_EPS
            return (num / den).reshape(B, N, C)

        def layer_norm(x, gamma, beta):
            mu = jnp.mean(x, axis=-1, keepdims=True)
            var = jnp.mean(jnp.square(x - mu), axis=-1, keepdims=True)
            return (x - mu) * lax.rsqrt(var + LN_EPS) * gamma + beta
        low = x
        highs = []
        lens = []
        for _ in range(NUM_LEVELS):
            lens.append(low.shape[1])
            l = dwconv(low, h_filter)[:, ::2]
            h = dwconv(low, g_filter)[:, ::2]
            highs.append(h)
            low = l
        low = linear_attention(low, NUM_HEADS)
        for h, L in zip(reversed(highs), reversed(lens)):
            up_l = jnp.repeat(low, 2, axis=1)[:, :L]
            up_h = jnp.repeat(h, 2, axis=1)[:, :L]
            low = dwconv(up_l, h_synth) + dwconv(up_h, g_synth)
        return layer_norm(x + low, norm_gamma, norm_beta)

    def _L0_ffn_ref(x, w_gate, w_up, w_down):
        import jax, jax.numpy as jnp
        import numpy as np
        DIM = 512
        HIDDEN = 1536
        SCALE = 1.0 / 127.0

        def _dequant(w_int, dtype):
            return w_int.astype(dtype) * jnp.asarray(SCALE, dtype)
        wg = _dequant(w_gate, x.dtype)
        wu = _dequant(w_up, x.dtype)
        wd = _dequant(w_down, x.dtype)
        gate = jnp.einsum('bsd,hd->bsh', x, wg)
        up = jnp.einsum('bsd,hd->bsh', x, wu)
        h = jax.nn.silu(gate) * up
        return jnp.einsum('bsh,dh->bsd', h, wd)
    x = L0_attn_x
    x = _layernorm(x + _L0_attn_ref(x, L0_attn_h_filter, L0_attn_g_filter, L0_attn_h_synth, L0_attn_g_synth, L0_attn_norm_gamma, L0_attn_norm_beta), axis=-1)
    x = _layernorm(x + _L0_ffn_ref(x, L0_ffn_w_gate, L0_ffn_w_up, L0_ffn_w_down), axis=-1)
    return x

_drawn_inputs = setup_inputs


def setup_inputs(seed=0):
    import zlib

    import numpy as np

    out = dict(_drawn_inputs(seed))
    spreads = {'L0_attn_norm_gamma': (1.0, 0.2), 'L0_attn_norm_beta': (0.0, 0.1)}
    factors = {}
    for name, (base, spread) in spreads.items():
        noise = np.random.default_rng([zlib.crc32(name.encode()), seed]).standard_normal(out[name].shape)
        drawn = base * np.exp(spread * noise) if base else spread * noise
        out[name] = jnp.asarray(drawn.astype(out[name].dtype))
    for name, factor in factors.items():
        out[name] = (out[name] * factor).astype(out[name].dtype)
    return out
```

```python
from contextlib import ExitStack

import concourse.bass as bass
from concourse import mybir

P = 128
BATCHES, SEQ, C = 2, 4096, 512
HID = 1536
NC = C // P
NH = HID // P
TOK = 1024
PER_BATCH = SEQ // TOK
ITERS = BATCHES * PER_BATCH
BLK = 512
SUBS = TOK // P
DSUB = BLK // P
M1 = TOK // 2
M2 = TOK // 4
XW = TOK + 6
LW = M1 + 2
QW = M2 + 3
HEAD = 32
LN_EPS = 1e-5
ATTN_EPS = 1e-6
X1_SCALE = 2048.0
H_SCALE = 0.125
WSCALE = 1.0 / 127.0
PIECES = 12
PW = HID

F32 = mybir.dt.float32
F16 = mybir.dt.float16
I32 = mybir.dt.int32
ALU = mybir.AluOpType
ACT = mybir.ActivationFunctionType

H0, G0, S0, T0 = 0, 4, 8, 12
S12, S01, S23, T12, T01, T23 = 16, 17, 18, 19, 20, 21
NCOEF = 22

NEXT, NOW, ANA = "next iteration", "this iteration", "analysis"
BESIDE = {
    (0, 0): [(NOW, "norm1", 4)],
    (0, 1): [(NOW, "norm2", 4), (ANA, "low1", 0)],
    (0, 2): [(NOW, "norm1", 5), (NOW, "normx", 4)],
    (0, 3): [(NOW, "norm2", 5), (NOW, "norm3", 4), (ANA, "low1", 1)],
    (0, 4): [(NOW, "norm1", 6), (NOW, "normx", 5)],
    (0, 5): [(NOW, "norm2", 6), (NOW, "norm3", 5), (ANA, "low1", 2)],
    (0, 6): [(NOW, "norm1", 7), (NOW, "normx", 6)],
    (0, 7): [(NOW, "norm2", 7), (NOW, "norm3", 6), (ANA, "low1", 3)],
    (0, 8): [(NOW, "normx", 7), (ANA, "band2", 0)],
    (0, 9): [(NOW, "norm3", 7), (ANA, "band2", 1)],
    (0, 10): [(ANA, "band2", 2), (ANA, "band2", 3), (ANA, "exp", 0)],
    (0, 11): [(ANA, "keys", 0), (ANA, "turn", 0), (ANA, "turn", 1), (ANA, "turn", 2), (ANA, "turn", 3)],
    (0, 12): [(NEXT, "high1", 0), (ANA, "kv", 0)],
    (0, 13): [(ANA, "blocks", 0), (NEXT, "high1", 1)],
    (0, 14): [(NEXT, "high1", 2), (NEXT, "high1", 3)],
    (0, 15): [(NEXT, "attend", 0), (NEXT, "synth2", 0)],
    (1, 0): [(NEXT, "synth1a", 0)],
    (1, 1): [(NEXT, "synth1b", 0)],
    (1, 2): [(NEXT, "attend", 1), (NEXT, "synth2", 1)],
    (1, 3): [(NEXT, "synth1a", 1)],
    (1, 4): [(NEXT, "synth1b", 1)],
    (1, 5): [(NEXT, "attend", 2), (NEXT, "synth2", 2)],
    (1, 6): [(NEXT, "synth1a", 2)],
    (1, 7): [(NEXT, "synth1b", 2)],
    (1, 8): [(NEXT, "attend", 3), (NEXT, "synth2", 3)],
    (1, 9): [(NEXT, "synth1a", 3)],
    (1, 10): [(NEXT, "synth1b", 3)],
    (1, 11): [(NEXT, "norm1", 0)],
    (1, 12): [(NEXT, "norm2", 0), (NEXT, "norm1", 1)],
    (1, 13): [(NEXT, "normx", 0), (NEXT, "norm2", 1), (NEXT, "norm1", 2)],
    (1, 14): [(NEXT, "norm3", 0), (NEXT, "normx", 1), (NEXT, "norm2", 2), (NEXT, "norm1", 3)],
    (1, 15): [(NEXT, "norm3", 1), (NEXT, "normx", 2), (NEXT, "norm2", 3), (NEXT, "norm3", 2),
              (NEXT, "normx", 3), (NEXT, "norm3", 3)],
}
FIRST_ANALYSIS = [("low1", 0), ("low1", 1), ("band2", 0), ("low1", 2), ("band2", 1), ("low1", 3),
                  ("band2", 2), ("band2", 3), ("exp", 0), ("keys", 0), ("turn", 0), ("turn", 1),
                  ("turn", 2), ("turn", 3), ("kv", 0)]
FIRST_MIX = [("high1", 0), ("high1", 1), ("attend", 0), ("high1", 2), ("high1", 3)]
for _c in range(NC):
    FIRST_MIX += [("synth2", _c)] + ([("attend", _c + 1)] if _c + 1 < NC else []) + \
                 [("synth1a", _c), ("synth1b", _c)]
FIRST_NORM = [("norm1", 0), ("norm2", 0), ("norm1", 1), ("normx", 0), ("norm2", 1), ("norm3", 0),
              ("norm1", 2), ("normx", 1), ("norm2", 2), ("norm3", 1), ("norm1", 3), ("normx", 2),
              ("norm2", 3), ("norm3", 2), ("normx", 3), ("norm3", 3)]

N_HIGH1, N_LOW1, N_BAND2, N_ATT, N_SYN2, N_SYN1, N_KEYS, N_BLOCKS = 4, 4, 7, 3, 9, 10, 5, 5


def mixer_ffn(nc, x_tok, x_chan, taps, gamma, beta, edge, weights, identity, block_mask, out):
    q_dram = nc.dram_tensor("q_scratch", [P, BATCHES, NC, SEQ // 4 + 3], F32, kind="Internal").ap()
    h2_dram = nc.dram_tensor("h2_scratch", [P, BATCHES, NC, SEQ // 4 + 3], F32, kind="Internal").ap()

    with ExitStack() as ctx:
        def sb(name, shape, dt=F32):
            return ctx.enter_context(nc.sbuf_tensor(name, shape, dt))

        def sem(name):
            return ctx.enter_context(nc.semaphore(name))

        w16 = sb("w16", [P, PIECES * PW], F16)
        coef = sb("coef", [P, NC, NCOEF])
        gamma_b = sb("gamma_b", [P, C])
        beta_b = sb("beta_b", [P, C])
        edge_sb = sb("edge_sb", [P, 2 * ITERS])
        ident = sb("ident", [P, P])
        mask = sb("mask", [P, P])
        zeros = sb("zeros", [P, 16])
        minus_half = sb("minus_half", [P, 1])
        eps1 = sb("eps1", [P, 1])
        xa = sb("xa", [P, NC, XW])
        l1 = sb("l1", [P, NC, LW])
        l2 = sb("l2", [P, NC, M2])
        h2 = sb("h2", [P, NC, M2])
        keys = sb("keys", [P, NC, M2])
        kv_sum = sb("kv_sum", [P, NC * P])
        z_part = sb("z_part", [P, NC])
        z_sum = sb("z_sum", [P, NC])
        kv_blocks = sb("kv_blocks", [P, NC, P])
        z_blocks = sb("z_blocks", [P, NC, P])
        xb = sb("xb", [P, NC, XW])
        q_in = sb("q_in", [P, NC, QW])
        h2_in = sb("h2_in", [P, NC, QW])
        h1_mem = sb("h1_mem", [P, NC * LW])
        h1 = h1_mem[:, :].rearrange("p (c n) -> p c n", c=NC)
        kvt = h1_mem[:, 0:NC * 4 * P].rearrange("p (c n) -> p c n", c=NC)
        low = sb("low", [P, 2, LW])
        att = sb("att", [P, 2, QW])
        xt = sb("xt", [P, 4, C])
        r = sb("r", [P, 2, C])
        x1 = sb("x1", [P, SUBS, C])
        st1 = sb("st1", [P, SUBS, 6])
        st2 = sb("st2", [P, SUBS, 6])
        mv1 = sb("mv1", [P, SUBS, 2])
        mv2 = sb("mv2", [P, SUBS, 2])
        rs1 = sb("rs1", [P, SUBS, 2])
        rs2 = sb("rs2", [P, SUBS, 4])
        x1_hi = sb("x1_hi", [P, 2, NC, BLK], F16)
        x1_lo = sb("x1_lo", [P, 2, NC, BLK], F16)
        hid = sb("hid", [P, 2 * NH * BLK], F16)
        h_hi = hid[:, 0:NH * BLK].rearrange("p (k n) -> p k n", k=NH)
        h_lo = hid[:, NH * BLK:2 * NH * BLK].rearrange("p (k n) -> p k n", k=NH)
        stage = hid[:, :].bitcast(I32)
        gate_s = sb("gate_s", [P, 2, BLK])
        h_f = sb("h_f", [P, 2, BLK])
        z = sb("z", [P, DSUB, C])
        st3 = sb("st3", [P, DSUB, 6])
        mv3 = sb("mv3", [P, DSUB, 2])
        rs3 = sb("rs3", [P, DSUB, 4])
        eps2 = sb("eps2", [P, 1])
        eps3 = sb("eps3", [P, 1])
        shrink = sb("shrink", [P, 1])
        minus_one = sb("minus_one", [P, 1])

        ps_gu = [[ctx.enter_context(nc.psum_tensor(f"ps_{n}{k}", [P, BLK], F32)) for n in ("gate", "up")]
                 for k in range(2)]
        ps_d = [ctx.enter_context(nc.psum_tensor(f"ps_down{k}", [P, C], F32)) for k in range(2)]
        ps_x = ctx.enter_context(nc.psum_tensor("ps_x", [P, 512], F32))
        ps_y = ctx.enter_context(nc.psum_tensor("ps_y", [P, 512], F32))

        ld_const, zero_pads = sem("ld_const"), sem("zero_pads")
        ld_w = [sem(f"ld_w{n}") for n in range(3)]
        ld_xa = [sem(f"ld_xa{c}") for c in range(NC)]
        ld_xb, ld_q, ld_h2 = sem("ld_xb"), sem("ld_q"), sem("ld_h2")
        ld_xt = [sem(f"ld_xt{n}") for n in range(4)]
        st_q, st_h2 = sem("st_q"), sem("st_h2")
        st_out = [sem(f"st_out{t}") for t in range(DSUB)]
        set_dve, set_pool, coef_ready, w_cast = sem("set_dve"), sem("set_pool"), sem("coef_ready"), sem("w_cast")
        sums_zero = sem("sums_zero")
        l1_first, band2_first, low1_step, band2_step = (sem("l1_first"), sem("band2_first"), sem("low1_step"),
                                                        sem("band2_step"))
        exp_done, keys_step, turned, turn_out = sem("exp_done"), sem("keys_step"), sem("turned"), sem("turn_out")
        kv_ready, kv_added, blocks_step = sem("kv_ready"), sem("kv_added"), sem("blocks_step")
        h1_first, low_first, high1_step = sem("h1_first"), sem("low_first"), sem("high1_step")
        qk_ready, att_step, syn2_step, syn1_step = sem("qk_ready"), sem("att_step"), sem("syn2_step"), sem("syn1_step")
        s_ready, s_stats, s_mv, s_centred = sem("s_ready"), sem("s_stats"), sem("s_mv"), sem("s_centred")
        var1_eps, rstd1, x_beta = sem("var1_eps"), sem("rstd1"), sem("x_beta")
        r_ready, r_stats, r_mv = sem("r_ready"), sem("r_stats"), sem("r_mv")
        var2_eps, var2_scaled, rstd2, nmean2, shift2 = (sem("var2_eps"), sem("var2_scaled"), sem("rstd2"),
                                                        sem("nmean2"), sem("shift2"))
        x1_ready, x1_turned, x1_hi_ready, x1_lo_ready = (sem("x1_ready"), sem("x1_turned"), sem("x1_hi_ready"),
                                                         sem("x1_lo_ready"))
        gu_ready, silu_done, h_mul, hi_done, lo_done = (sem("gu_ready"), sem("silu_done"), sem("h_mul"),
                                                        sem("hi_done"), sem("lo_done"))
        d_ready, z_done, z_stats, z_mv = sem("d_ready"), sem("z_done"), sem("z_stats"), sem("z_mv")
        var3_eps, rstd3, nmean3, shift3, out_done = (sem("var3_eps"), sem("rstd3"), sem("nmean3"), sem("shift3"),
                                                     sem("out_done"))

        def hold(eng, semaphore, value):
            eng.wait_ge(semaphore, value)
            eng.nop(nofuse=True)

        def analyses(eng, body):
            body(0)
            with eng.Fori(1, PER_BATCH) as a:
                body(a)

        def first(index):
            return isinstance(index, int) and index == 0

        def iterations(eng, body):
            with eng.Fori(0, PER_BATCH - 1) as i:
                body(i, 0, True, False)
            body(PER_BATCH - 1, 0, True, True)
            with eng.Fori(PER_BATCH, ITERS - 1) as i:
                body(i, 1, False, False)
            body(ITERS - 1, 1, False, True)

        def beside(b, k, i, batch, analysis, last, steps):
            for which, name, n in BESIDE[(b, k)]:
                if name not in steps:
                    continue
                if which is NOW:
                    steps[name](i, batch, n)
                elif which is NEXT and not (last and batch == 1):
                    steps[name](i + 1, batch + (1 if last else 0), n)
                elif which is ANA and analysis and (name != "blocks" or last):
                    steps[name](i + PER_BATCH, 1, n)

        block = ctx.enter_context(nc.Block())

        @block.sync
        def _(sp):
            for dst, src in ((coef[:, :, 0:16], taps), (gamma_b[:, :], gamma), (beta_b[:, :], beta),
                             (edge_sb[:, :], edge), (ident[:, :], identity), (mask[:, :], block_mask)):
                sp.dma_start(dst, src).then_inc(ld_const, 16)

            def load_xa(a, batch, c):
                sp.dma_start(xa[:, c, :], x_chan[:, batch, c, bass.ds((a - PER_BATCH * batch) * TOK, XW)]
                             ).then_inc(ld_xa[c], 16)

            def low1(a, batch, c):
                if isinstance(a, int) and a == ITERS - 1:
                    return
                hold(sp, low1_step, (a * NC + c) * N_LOW1 + 3)
                load_xa(a + 1, batch, c)

            def keys_store(a, batch, _):
                at = (a - PER_BATCH * batch) * M2 + 1
                hold(sp, band2_step, (a + 1) * NC * N_BAND2)
                sp.dma_start(h2_dram[:, batch, :, bass.ds(at, M2)], h2[:, :, :]).then_inc(st_h2, 16)
                hold(sp, keys_step, (a + 1) * N_KEYS)
                sp.dma_start(q_dram[:, batch, :, bass.ds(at, M2)], keys[:, :, :]).then_inc(st_q, 16)

            def load_xb(j, batch):
                sp.dma_start(xb[:, :, :], x_chan[:, batch, :, bass.ds((j - PER_BATCH * batch) * TOK, XW)]
                             ).then_inc(ld_xb, 16)

            def load_bands(j, batch):
                at = (j - PER_BATCH * batch) * M2
                hold(sp, st_q, 16 * PER_BATCH * (batch + 1))
                hold(sp, st_h2, 16 * PER_BATCH * (batch + 1))
                sp.dma_start(q_in[:, :, :], q_dram[:, batch, :, bass.ds(at, QW)]).then_inc(ld_q, 16)
                sp.dma_start(h2_in[:, :, :], h2_dram[:, batch, :, bass.ds(at, QW)]).then_inc(ld_h2, 16)

            def load_xt(j, batch, t):
                sp.dma_start(xt[:, t % 4, :], x_tok[batch, bass.ds((j - PER_BATCH * batch) * TOK + t * P, P), :]
                             ).then_inc(ld_xt[t % 4], 16)

            for c in range(NC):
                load_xa(0, 0, c)
            hold(sp, set_dve, 1)
            for dram in (q_dram, h2_dram):
                for at, width in ((0, 1), (SEQ // 4 + 1, 2)):
                    sp.dma_start(dram[:, :, :, at:at + width], zeros[:, 0:8 * width].rearrange(
                        "p (b c w) -> p b c w", b=BATCHES, c=NC), allow_slow_non_contiguous=True
                        ).then_inc(zero_pads, 16)
            def analysis(a):
                for n in range(3):
                    if not first(a):
                        hold(sp, w_cast, 3 * a)
                    sp.dma_start(stage[:, n * PW:(n + 1) * PW], weights[:, bass.ds((a * 3 + n) * PW, PW)]
                                 ).then_inc(ld_w[n], 16)
                for c in range(NC):
                    hold(sp, low1_step, (a * NC + c) * N_LOW1 + 3)
                    sp.dma_start(xa[:, c, :], x_chan[:, 0, c, bass.ds((a + 1) * TOK, XW)]).then_inc(ld_xa[c], 16)
                keys_store(a, 0, 0)

            analyses(sp, analysis)
            hold(sp, zero_pads, 64)
            load_xb(0, 0)
            load_bands(0, 0)
            for t in range(4):
                load_xt(0, 0, t)
            for c in range(NC):
                hold(sp, ld_xa[c], 16 * (PER_BATCH + 1))
                load_xa(PER_BATCH, 1, c)

            def after_norm2(j, batch, t):
                if isinstance(j, int) and j == ITERS - 1 and t >= 4:
                    return
                hold(sp, r_ready, SUBS * j + t + 1)
                if t < 4:
                    load_xt(j, batch, t + 4)
                elif isinstance(j, int):
                    load_xt(j + 1, batch + 1, t - 4)
                else:
                    load_xt(j + 1, batch, t - 4)

            steps = {"low1": low1, "keys": keys_store, "norm2": after_norm2}
            for t in range(4):
                after_norm2(0, 0, t)

            def body(i, batch, analysis, last):
                more = not (last and batch == 1)
                nb = batch + (1 if last else 0)
                for b in range(2):
                    for k in range(NH + DSUB):
                        beside(b, k, i, batch, analysis, last, steps)
                        if (b, k) == (0, 7) and more:
                            hold(sp, s_ready, SUBS * (i + 1))
                            load_xb(i + 1, nb)
                        if (b, k) == (0, 12) and more:
                            hold(sp, syn2_step, N_SYN2 * NC * (i + 1))
                            load_bands(i + 1, nb)
                        if k >= NH:
                            t = k - NH
                            B = 2 * i + b
                            hold(sp, out_done, DSUB * B + t + 1)
                            sp.dma_start(out[batch, bass.ds((i - PER_BATCH * batch) * TOK + b * BLK + t * P, P), :],
                                         z[:, t, :]).then_inc(st_out[t], 16)

            iterations(sp, body)
            for t in range(DSUB):
                hold(sp, st_out[t], 16 * (2 * ITERS + 1))

        @block.tensor
        def _(pe):
            def turn(a, batch, c):
                bank = (ps_x, ps_y)[c % 2]
                if c == 0:
                    pe.wait_ge(keys_step, (a + 1) * N_KEYS - 1)
                    if not first(a):
                        pe.wait_ge(kv_added, a)
                    if batch == 1:
                        pe.wait_ge(x1_lo_ready, SUBS * (a - PER_BATCH + 1))
                if c >= 2:
                    pe.wait_ge(turn_out, NC * a + c - 1)
                for n, src in enumerate((keys[:, c, 0:P], keys[:, c, P:2 * P], l2[:, c, 0:P], l2[:, c, P:2 * P])):
                    mm = pe.transpose(bank[:, n * P:(n + 1) * P], src, ident[:, :])
                mm.then_inc(turned, 1)

            def kv(a, batch, _):
                pe.wait_ge(turn_out, NC * (a + 1))
                for c in range(NC):
                    for n in range(2):
                        mm = pe.matmul(ps_x[:, c * P:(c + 1) * P], kvt[:, c, n * P:(n + 1) * P],
                                       kvt[:, c, (2 + n) * P:(3 + n) * P], start=(n == 0), stop=(n == 1))
                mm.then_inc(kv_ready, 1)

            def attend(j, batch, c):
                if c == 0:
                    pe.wait_ge(ld_q, 16 * (j + 1))
                    pe.wait_ge(blocks_step, N_BLOCKS * (batch + 1))
                    if isinstance(j, int) and j == 0:
                        pe.wait_ge(turn_out, NC * PER_BATCH)
                    elif batch == 0 or isinstance(j, int):
                        pe.wait_ge(kv_added, j + PER_BATCH)
                    else:
                        pe.wait_ge(x1_lo_ready, SUBS * j)
                else:
                    pe.wait_ge(att_step, N_ATT * (NC * j + c))
                pe.matmul(ps_y[:, 0:QW], z_blocks[:, c, :], q_in[:, c, :], start=True, stop=True)
                pe.matmul(ps_x[:, 0:QW], kv_blocks[:, c, :], q_in[:, c, :], start=True, stop=True
                          ).then_inc(qk_ready, 1)

            def norm1(j, batch, t):
                if t == 0:
                    pe.wait_ge(syn1_step, N_SYN1 * NC * (j + 1))
                    pe.wait_ge(att_step, N_ATT * NC * (j + 1))
                else:
                    pe.wait_ge(s_centred, SUBS * j + t)
                for c in range(NC):
                    mm = pe.transpose(ps_x[:, c * P:(c + 1) * P], xb[:, c, 3 + t * P:3 + (t + 1) * P], ident[:, :])
                mm.then_inc(s_ready, 1)

            def norm3(j, batch, t):
                s = SUBS * j + t
                pe.wait_ge(x1_ready, s + 1)
                if not (isinstance(j, int) and s == 0):
                    pe.wait_ge(x1_lo_ready, s)
                for c in range(NC):
                    mm = pe.transpose(ps_y[:, c * P:(c + 1) * P], x1[:, t, c * P:(c + 1) * P], ident[:, :])
                mm.then_inc(x1_turned, 1)

            steps = {"turn": turn, "kv": kv, "attend": attend, "norm1": norm1, "norm3": norm3}

            def gate_up(B, b, k):
                if k == 0:
                    pe.wait_ge(x1_hi_ready, DSUB * (B + 1))
                    pe.wait_ge(x1_lo_ready, DSUB * (B + 1))
                pe.wait_ge(h_mul, NH * B + k + 1)
                for g in range(2):
                    for c in range(NC):
                        w = w16[:, (g * NC + c) * PW + k * P:(g * NC + c) * PW + (k + 1) * P]
                        pe.matmul(ps_gu[k % 2][g][:, :], w, x1_hi[:, b, c, :], start=(c == 0), stop=False)
                        mm = pe.matmul(ps_gu[k % 2][g][:, :], w, x1_lo[:, b, c, :], start=False, stop=(c == NC - 1))
                mm.then_inc(gu_ready, 1)

            def down(B, t):
                if t == 0:
                    pe.wait_ge(hi_done, NH * (B + 1))
                    pe.wait_ge(lo_done, NH * (B + 1))
                pe.wait_ge(z_done, DSUB * B + t + 1)
                for k in range(NH):
                    w = w16[:, 2 * NC * PW + k * C:2 * NC * PW + (k + 1) * C]
                    pe.matmul(ps_d[t % 2][:, :], h_hi[:, k, t * P:(t + 1) * P], w, start=(k == 0), stop=False)
                    mm = pe.matmul(ps_d[t % 2][:, :], h_lo[:, k, t * P:(t + 1) * P], w, start=False,
                                   stop=(k == NH - 1))
                mm.then_inc(d_ready, 1)

            def body(i, batch, analysis, last):
                for b in range(2):
                    for k in range(NH):
                        gate_up(2 * i + b, b, k)
                        beside(b, k, i, batch, analysis, last, steps)
                    for t in range(DSUB):
                        down(2 * i + b, t)
                        beside(b, NH + t, i, batch, analysis, last, steps)

            pe.wait_ge(ld_const, 96)
            def analysis(a):
                for name, n in FIRST_ANALYSIS:
                    if name in steps:
                        steps[name](a, 0, n)

            analyses(pe, analysis)
            for name, n in FIRST_MIX + FIRST_NORM:
                if name in steps:
                    steps[name](0, 0, n)
            pe.wait_ge(w_cast, PIECES)
            iterations(pe, body)

        @block.scalar
        def _(act):
            def first_tap(dst, src, c, tap, done):
                nc.scalar.activation(dst, src, ACT.Copy, scale=coef[:, c, tap:tap + 1]).then_inc(done, 1)

            def low1(a, batch, c):
                act.wait_ge(ld_xa[c], 16 * (a + 1) + (16 if batch == 1 else 0))
                if not first(a):
                    act.wait_ge(band2_step, NC * N_BAND2 * a)
                first_tap(l1[:, c, :], xa[:, c, 0:2 * LW - 1:2], c, H0, l1_first)

            def band2(a, batch, c):
                act.wait_ge(low1_step, (NC * a + c + 1) * N_LOW1)
                if c == 0 and not first(a):
                    act.wait_ge(keys_step, N_KEYS * a)
                    act.wait_ge(turned, NC * a)
                    act.wait_ge(st_h2, 16 * a)
                first_tap(l2[:, c, :], l1[:, c, 0:2 * M2 - 1:2], c, H0, band2_first)
                first_tap(h2[:, c, :], l1[:, c, 0:2 * M2 - 1:2], c, G0, band2_first)

            def exp(a, batch, _):
                act.wait_ge(band2_step, NC * N_BAND2 * (a + 1))
                nc.scalar.activation(keys[:, :, :], keys[:, :, :], ACT.Exp).then_inc(exp_done, 1)

            def turn(a, batch, c):
                act.wait_ge(turned, NC * a + c + 1)
                if c == 0:
                    if batch == 1:
                        act.wait_ge(syn1_step, N_SYN1 * NC * (a - PER_BATCH + 1))
                    if not first(a):
                        act.wait_ge(kv_ready, a)
                nc.scalar.activation(kvt[:, c, :], (ps_x, ps_y)[c % 2][:, :], ACT.Copy).then_inc(turn_out, 1)

            def high1(j, batch, c):
                if c == 0:
                    act.wait_ge(ld_xb, 16 * (j + 1))
                    if not first(j):
                        act.wait_ge(syn1_step, N_SYN1 * NC * j)
                    if batch == 0 or isinstance(j, int):
                        act.wait_ge(kv_ready, PER_BATCH if isinstance(j, int) and j == 0 else j + PER_BATCH)
                first_tap(h1[:, c, :], xb[:, c, 0:2 * LW - 1:2], c, G0, h1_first)

            def synth2(j, batch, c):
                if c == 0:
                    act.wait_ge(ld_h2, 16 * (j + 1))
                if not (isinstance(j, int) and NC * j + c < 2):
                    act.wait_ge(syn1_step, N_SYN1 * (NC * j + c - 1))
                u = M2 + 1
                first_tap(low[:, c % 2, 0:2 * u - 1:2], h2_in[:, c, 0:u], c, T01, low_first)
                first_tap(low[:, c % 2, 1:2 * u:2], h2_in[:, c, 0:u], c, T0, low_first)

            def normx(j, batch, t):
                act.wait_ge(rstd2, SUBS * j + t + 1)
                act.wait_ge(shift2, SUBS * j + t + 1)
                nc.scalar.activation(x1[:, t, :], r[:, t % 2, :], ACT.Identity, bias=rs2[:, t, 3:4],
                                     scale=rs2[:, t, 1:2]).then_inc(x1_ready, 1)

            def norm3(j, batch, t):
                act.wait_ge(x1_turned, SUBS * j + t + 1)
                nc.scalar.activation(x1_hi[:, t // DSUB, :, (t % DSUB) * P:(t % DSUB + 1) * P],
                                     ps_y[:, :].rearrange("p (c n) -> p c n", c=NC), ACT.Copy
                                     ).then_inc(x1_hi_ready, 1)

            steps = {"low1": low1, "band2": band2, "exp": exp, "turn": turn, "high1": high1, "synth2": synth2,
                     "normx": normx, "norm3": norm3}

            act.wait_ge(coef_ready, 6)
            def analysis(a):
                for name, n in FIRST_ANALYSIS:
                    if name in steps:
                        steps[name](a, 0, n)
                    if name == "low1" and n > 0:
                        act.wait_ge(ld_w[n - 1], 16 * (a + 1))
                        nc.scalar.activation(w16[:, bass.ds((a * 3 + n - 1) * PW, PW)],
                                             stage[:, (n - 1) * PW:n * PW], ACT.Copy).then_inc(w_cast, 1)

            analyses(act, analysis)
            for name, n in FIRST_MIX + FIRST_NORM:
                if name in steps:
                    steps[name](0, 0, n)

            def body(i, batch, analysis, last):
                for b in range(2):
                    B = 2 * i + b
                    for k in range(NH):
                        act.wait_ge(gu_ready, NH * B + k + 1)
                        nc.scalar.activation(gate_s[:, k % 2, :], ps_gu[k % 2][0][:, :], ACT.Silu,
                                             scale=WSCALE / X1_SCALE).then_inc(silu_done, 1)
                        beside(b, k, i, batch, analysis, last, steps)
                        act.wait_ge(h_mul, NH * B + k + 3)
                        nc.scalar.activation(h_hi[:, k, :], h_f[:, k % 2, :], ACT.Copy).then_inc(hi_done, 1)
                    for t in range(DSUB):
                        beside(b, NH + t, i, batch, analysis, last, steps)
                        act.wait_ge(rstd3, DSUB * B + t + 1)
                        act.wait_ge(shift3, DSUB * B + t + 1)
                        nc.scalar.activation(z[:, t, :], z[:, t, :], ACT.Identity, bias=rs3[:, t, 2:3],
                                             scale=rs3[:, t, 1:2]).then_inc(out_done, 1)

            iterations(act, body)

        @block.gpsimd
        def _(pool):
            nc.gpsimd.memset(minus_half[:], -0.5).then_inc(set_pool, 1)
            nc.gpsimd.memset(minus_one[:], -1.0).then_inc(set_pool, 1)
            nc.gpsimd.memset(eps1[:], LN_EPS).then_inc(set_pool, 1)
            nc.gpsimd.memset(eps3[:], LN_EPS * X1_SCALE * X1_SCALE).then_inc(set_pool, 1)
            nc.gpsimd.memset(shrink[:], X1_SCALE ** -2).then_inc(set_pool, 1)
            pool.wait_ge(set_pool, 5)
            pool.wait_ge(ld_const, 96)

            def norm1(j, batch, t):
                s = SUBS * j + t
                pool.wait_ge(s_mv, s + 1)
                nc.gpsimd.tensor_tensor(rs1[:, t, 0:1], mv1[:, t, 1:2], eps1[:, :], ALU.add).then_inc(var1_eps, 1)
                pool.wait_ge(var1_eps, s + 1)
                nc.gpsimd.tensor_tensor(rs1[:, t, 1:2], rs1[:, t, 0:1], minus_half[:, :], ALU.pow
                                        ).then_inc(rstd1, 1)

            def xbeta(j, batch, t):
                pool.wait_ge(ld_xt[t % 4], 16 * (2 * j + t // 4 + 1))
                nc.gpsimd.tensor_tensor(xt[:, t % 4, :], xt[:, t % 4, :], beta_b[:, :], ALU.add
                                        ).then_inc(x_beta, 1)

            def norm1_and_x(j, batch, t):
                xbeta(j, batch, t)
                norm1(j, batch, t)

            def norm2(j, batch, t):
                s = SUBS * j + t
                pool.wait_ge(r_mv, s + 1)
                nc.gpsimd.tensor_tensor(rs2[:, t, 0:1], mv2[:, t, 1:2], eps1[:, :], ALU.add).then_inc(var2_eps, 1)
                nc.gpsimd.tensor_tensor(rs2[:, t, 2:3], mv2[:, t, 0:1], minus_one[:, :], ALU.mult
                                        ).then_inc(nmean2, 1)
                pool.wait_ge(var2_eps, s + 1)
                nc.gpsimd.tensor_tensor(rs2[:, t, 0:1], rs2[:, t, 0:1], shrink[:, :], ALU.mult
                                        ).then_inc(var2_scaled, 1)
                pool.wait_ge(var2_scaled, s + 1)
                nc.gpsimd.tensor_tensor(rs2[:, t, 1:2], rs2[:, t, 0:1], minus_half[:, :], ALU.pow
                                        ).then_inc(rstd2, 1)
                pool.wait_ge(rstd2, s + 1)
                pool.wait_ge(nmean2, s + 1)
                nc.gpsimd.tensor_tensor(rs2[:, t, 3:4], rs2[:, t, 2:3], rs2[:, t, 1:2], ALU.mult
                                        ).then_inc(shift2, 1)

            steps = {"norm1": norm1_and_x, "norm2": norm2}
            for name, n in FIRST_NORM:
                if name in steps:
                    steps[name](0, 0, n)

            def body(i, batch, analysis, last):
                for b in range(2):
                    for k in range(NH + DSUB):
                        beside(b, k, i, batch, analysis, last, steps)
                        if k >= NH:
                            t = k - NH
                            n = DSUB * (2 * i + b) + t
                            pool.wait_ge(z_mv, n + 1)
                            nc.gpsimd.tensor_tensor(rs3[:, t, 0:1], mv3[:, t, 1:2], eps3[:, :], ALU.add
                                                    ).then_inc(var3_eps, 1)
                            nc.gpsimd.tensor_tensor(rs3[:, t, 3:4], mv3[:, t, 0:1], minus_one[:, :], ALU.mult
                                                    ).then_inc(nmean3, 1)
                            pool.wait_ge(var3_eps, n + 1)
                            nc.gpsimd.tensor_tensor(rs3[:, t, 1:2], rs3[:, t, 0:1], minus_half[:, :], ALU.pow
                                                    ).then_inc(rstd3, 1)
                            pool.wait_ge(rstd3, n + 1)
                            pool.wait_ge(nmean3, n + 1)
                            nc.gpsimd.tensor_tensor(rs3[:, t, 2:3], rs3[:, t, 3:4], rs3[:, t, 1:2], ALU.mult
                                                    ).then_inc(shift3, 1)

            iterations(pool, body)

        @block.vector
        def _(dve):
            V = nc.vector
            V.memset(zeros[:], 0.0).then_inc(set_dve, 1)
            V.memset(kv_sum[:], 0.0).then_inc(h_mul, 2)
            V.memset(z_sum[:], 0.0).then_inc(z_done, 2)
            dve.wait_ge(ld_const, 96)
            for dst, a, b in ((S12, S0 + 1, S0 + 2), (S01, S0, S0 + 1), (S23, S0 + 2, S0 + 3),
                              (T12, T0 + 1, T0 + 2), (T01, T0, T0 + 1), (T23, T0 + 2, T0 + 3)):
                V.tensor_tensor(coef[:, :, dst:dst + 1], coef[:, :, a:a + 1], coef[:, :, b:b + 1], ALU.add
                                ).then_inc(coef_ready, 1)
            dve.wait_ge(coef_ready, 6)
            for t in range(DSUB):
                V.memset(z[:, t, 0:1], 0.0).then_inc(st_out[t], 16)

            def tap(acc, src, c, n, add=None):
                return V.scalar_tensor_tensor(out=acc, in0=src, scalar=coef[:, c, n:n + 1],
                                              in1=acc if add is None else add, op0=ALU.mult, op1=ALU.add)

            def edges(band, j):
                return V.tensor_tensor(band[:, 0:LW:LW - 1], band[:, 0:LW:LW - 1],
                                       edge_sb[:, bass.ds(2 * j, 2)], ALU.mult)

            def low1(a, batch, c):
                n = (NC * a + c) * N_LOW1
                dve.wait_ge(l1_first, NC * a + c + 1)
                for k in range(1, 4):
                    if k > 1:
                        dve.wait_ge(low1_step, n + k - 1)
                    tap(l1[:, c, :], xa[:, c, k:k + 2 * LW - 1:2], c, H0 + k).then_inc(low1_step, 1)
                dve.wait_ge(low1_step, n + 3)
                edges(l1[:, c, :], a).then_inc(low1_step, 1)

            def band2(a, batch, c):
                n = (NC * a + c) * N_BAND2
                dve.wait_ge(low1_step, (NC * a + c + 1) * N_LOW1)
                dve.wait_ge(band2_first, 2 * (NC * a + c + 1))
                for k in range(1, 4):
                    for which, (band, g) in enumerate(((l2, H0), (h2, G0))):
                        if k > 1:
                            dve.wait_ge(band2_step, n + 2 * (k - 1) + which - 1)
                        tap(band[:, c, :], l1[:, c, k:k + 2 * M2 - 1:2], c, g + k).then_inc(band2_step, 1)
                dve.wait_ge(band2_step, n + 5)
                if c == 0 and not first(a):
                    dve.wait_ge(turned, NC * a)
                    dve.wait_ge(st_q, 16 * a)
                V.tensor_scalar(keys[:, c, :], l2[:, c, :], 0.0, None, ALU.min).then_inc(band2_step, 1)

            def keys_sum(a, batch, _):
                dve.wait_ge(exp_done, a + 1)
                for c in range(NC):
                    V.scalar_tensor_tensor(out=keys[:, c, :], in0=l2[:, c, :], scalar=0.0, in1=keys[:, c, :],
                                           op0=ALU.max, op1=ALU.add, accum_out=z_part[:, c:c + 1]
                                           ).then_inc(keys_step, 1)
                dve.wait_ge(keys_step, N_KEYS * a + NC)
                V.tensor_tensor(z_sum[:, :], z_sum[:, :], z_part[:, :], ALU.add).then_inc(keys_step, 1)

            def kv(a, batch, _):
                dve.wait_ge(kv_ready, a + 1)
                V.tensor_tensor(kv_sum[:, :], ps_x[:, :], kv_sum[:, :], ALU.add).then_inc(kv_added, 1)

            def blocks(a, batch, _):
                dve.wait_ge(kv_added, PER_BATCH * (batch + 1))
                V.tensor_tensor(kv_blocks[:, :, :], kv_sum[:, :].rearrange("p (c n) -> p c n", c=NC),
                                mask[:, None, :].to_broadcast([P, NC, P]), ALU.mult).then_inc(blocks_step, 1)
                dve.wait_ge(keys_step, N_KEYS * PER_BATCH * (batch + 1))
                for c in range(NC):
                    V.tensor_scalar(z_blocks[:, c, :], mask[:, :], z_sum[:, c:c + 1], None, ALU.mult
                                    ).then_inc(blocks_step, 1)

            def high1(j, batch, c):
                n = (NC * j + c) * N_HIGH1
                dve.wait_ge(h1_first, NC * j + c + 1)
                for k in range(1, 4):
                    if k > 1:
                        dve.wait_ge(high1_step, n + k - 1)
                    tap(h1[:, c, :], xb[:, c, k:k + 2 * LW - 1:2], c, G0 + k).then_inc(high1_step, 1)
                dve.wait_ge(high1_step, n + 3)
                edges(h1[:, c, :], j).then_inc(high1_step, 1)

            def attend(j, batch, c):
                n = (NC * j + c) * N_ATT
                dve.wait_ge(qk_ready, NC * j + c + 1)
                V.tensor_scalar(att[:, c % 2, :], ps_y[:, 0:QW], ATTN_EPS, None, ALU.add).then_inc(att_step, 1)
                dve.wait_ge(att_step, n + 1)
                V.reciprocal(att[:, c % 2, :], att[:, c % 2, :]).then_inc(att_step, 1)
                dve.wait_ge(att_step, n + 2)
                V.tensor_tensor(att[:, c % 2, :], ps_x[:, 0:QW], att[:, c % 2, :], ALU.mult).then_inc(att_step, 1)

            def synth2(j, batch, c):
                n = (NC * j + c) * N_SYN2
                u = M2 + 1
                a_, h_ = att[:, c % 2, :], h2_in[:, c, :]
                odd, even = low[:, c % 2, 0:2 * u - 1:2], low[:, c % 2, 1:2 * u:2]
                dve.wait_ge(low_first, 2 * (NC * j + c + 1))
                tap(even, h_[:, 1:1 + u], c, T12).then_inc(syn2_step, 1)
                tap(odd, h_[:, 1:1 + u], c, T23).then_inc(syn2_step, 1)
                dve.wait_ge(syn2_step, n + 1)
                tap(even, h_[:, 2:2 + u], c, T0 + 3).then_inc(syn2_step, 1)
                dve.wait_ge(att_step, (NC * j + c + 1) * N_ATT)
                dve.wait_ge(syn2_step, n + 2)
                tap(odd, a_[:, 0:u], c, S01).then_inc(syn2_step, 1)
                dve.wait_ge(syn2_step, n + 3)
                tap(even, a_[:, 0:u], c, S0).then_inc(syn2_step, 1)
                dve.wait_ge(syn2_step, n + 4)
                tap(odd, a_[:, 1:1 + u], c, S23).then_inc(syn2_step, 1)
                dve.wait_ge(syn2_step, n + 5)
                tap(even, a_[:, 1:1 + u], c, S12).then_inc(syn2_step, 1)
                dve.wait_ge(syn2_step, n + 7)
                tap(even, a_[:, 2:2 + u], c, S0 + 3).then_inc(syn2_step, 1)
                dve.wait_ge(syn2_step, n + 8)
                edges(low[:, c % 2, :], j).then_inc(syn2_step, 1)

            def synth1a(j, batch, c):
                n = (NC * j + c) * N_SYN1
                even, odd = xb[:, c, 3:3 + TOK - 1:2], xb[:, c, 4:4 + TOK - 1:2]
                dve.wait_ge(high1_step, (NC * j + c + 1) * N_HIGH1)
                tap(even, h1[:, c, 0:M1], c, T0).then_inc(syn1_step, 1)
                tap(odd, h1[:, c, 1:1 + M1], c, T01).then_inc(syn1_step, 1)
                dve.wait_ge(syn1_step, n + 1)
                tap(even, h1[:, c, 1:1 + M1], c, T12).then_inc(syn1_step, 1)
                dve.wait_ge(syn1_step, n + 2)
                tap(odd, h1[:, c, 2:2 + M1], c, T23).then_inc(syn1_step, 1)
                dve.wait_ge(syn1_step, n + 3)
                tap(even, h1[:, c, 2:2 + M1], c, T0 + 3).then_inc(syn1_step, 1)

            def synth1b(j, batch, c):
                n = (NC * j + c) * N_SYN1
                even, odd = xb[:, c, 3:3 + TOK - 1:2], xb[:, c, 4:4 + TOK - 1:2]
                lw = low[:, c % 2, :]
                dve.wait_ge(syn2_step, (NC * j + c + 1) * N_SYN2)
                dve.wait_ge(syn1_step, n + 4)
                tap(odd, lw[:, 1:1 + M1], c, S01).then_inc(syn1_step, 1)
                dve.wait_ge(syn1_step, n + 5)
                tap(even, lw[:, 0:M1], c, S0).then_inc(syn1_step, 1)
                dve.wait_ge(syn1_step, n + 6)
                tap(odd, lw[:, 2:2 + M1], c, S23).then_inc(syn1_step, 1)
                dve.wait_ge(syn1_step, n + 7)
                tap(even, lw[:, 1:1 + M1], c, S12).then_inc(syn1_step, 1)
                dve.wait_ge(syn1_step, n + 9)
                tap(even, lw[:, 2:2 + M1], c, S0 + 3).then_inc(syn1_step, 1)

            def aggregate(dst, src, stats, value):
                hold(dve, stats, value)
                return V.bn_aggr(dst, src)

            def norm1(j, batch, t):
                s = SUBS * j + t
                dve.wait_ge(s_ready, s + 1)
                V.bn_stats(st1[:, t, :], ps_x[:, :]).then_inc(s_stats, 1)
                aggregate(mv1[:, t, :], st1[:, t, :], s_stats, s + 1).then_inc(s_mv, 1)
                dve.wait_ge(s_mv, s + 1)
                if not (isinstance(j, int) and s < 2):
                    dve.wait_ge(x1_ready, s - 1)
                V.scalar_tensor_tensor(out=r[:, t % 2, :], in0=ps_x[:, :], scalar=mv1[:, t, 0:1],
                                       in1=gamma_b[:, :], op0=ALU.subtract, op1=ALU.mult).then_inc(s_centred, 1)

            def norm2(j, batch, t):
                s = SUBS * j + t
                dve.wait_ge(s_centred, s + 1)
                dve.wait_ge(x_beta, s + 1)
                dve.wait_ge(rstd1, s + 1)
                V.scalar_tensor_tensor(out=r[:, t % 2, :], in0=r[:, t % 2, :], scalar=rs1[:, t, 1:2],
                                       in1=xt[:, t % 4, :], op0=ALU.mult, op1=ALU.add).then_inc(r_ready, 1)
                dve.wait_ge(r_ready, s + 1)
                V.bn_stats(st2[:, t, :], r[:, t % 2, :]).then_inc(r_stats, 1)
                aggregate(mv2[:, t, :], st2[:, t, :], r_stats, s + 1).then_inc(r_mv, 1)

            def norm3(j, batch, t):
                dve.wait_ge(x1_hi_ready, SUBS * j + t + 1)
                cols = slice((t % DSUB) * P, (t % DSUB + 1) * P)
                V.tensor_tensor(x1_lo[:, t // DSUB, :, cols], ps_y[:, :].rearrange("p (c n) -> p c n", c=NC),
                                x1_hi[:, t // DSUB, :, cols], ALU.subtract).then_inc(x1_lo_ready, 1)

            steps = {"low1": low1, "band2": band2, "keys": keys_sum, "kv": kv, "blocks": blocks, "high1": high1,
                     "attend": attend, "synth2": synth2, "synth1a": synth1a, "synth1b": synth1b,
                     "norm1": norm1, "norm2": norm2, "norm3": norm3}

            def analysis(a):
                for name, n in FIRST_ANALYSIS:
                    if name in steps:
                        steps[name](a, 0, n)

            analyses(dve, analysis)
            blocks(PER_BATCH - 1, 0, 0)
            dve.wait_ge(blocks_step, N_BLOCKS)
            V.memset(kv_sum[:], 0.0).then_inc(sums_zero, 1)
            V.memset(z_sum[:], 0.0).then_inc(sums_zero, 1)
            dve.wait_ge(sums_zero, 2)
            for name, n in FIRST_MIX + FIRST_NORM:
                if name in steps:
                    steps[name](0, 0, n)

            def body(i, batch, analysis, last):
                for b in range(2):
                    B = 2 * i + b
                    for k in range(NH):
                        n = NH * B + k
                        dve.wait_ge(silu_done, n + 1)
                        V.scalar_tensor_tensor(out=h_f[:, k % 2, :], in0=ps_gu[k % 2][1][:, :],
                                               scalar=WSCALE * H_SCALE / X1_SCALE, in1=gate_s[:, k % 2, :],
                                               op0=ALU.mult, op1=ALU.mult).then_inc(h_mul, 1)
                        beside(b, k, i, batch, analysis, last, steps)
                        dve.wait_ge(hi_done, n + 1)
                        V.tensor_tensor(h_lo[:, k, :], h_f[:, k % 2, :], h_hi[:, k, :], ALU.subtract
                                        ).then_inc(lo_done, 1)
                    for t in range(DSUB):
                        n = DSUB * B + t
                        if t == 0:
                            beside(b, NH + t, i, batch, analysis, last, steps)
                        dve.wait_ge(d_ready, n + 1)
                        dve.wait_ge(st_out[t], 16 * (B + 1))
                        V.scalar_tensor_tensor(out=z[:, t, :], in0=ps_d[t % 2][:, :],
                                               scalar=WSCALE * X1_SCALE / H_SCALE, in1=x1[:, b * DSUB + t, :],
                                               op0=ALU.mult, op1=ALU.add).then_inc(z_done, 1)
                        dve.wait_ge(z_done, n + 3)
                        V.bn_stats(st3[:, t, :], z[:, t, :]).then_inc(z_stats, 1)
                        aggregate(mv3[:, t, :], st3[:, t, :], z_stats, n + 1).then_inc(z_mv, 1)
                        if t > 0:
                            beside(b, NH + t, i, batch, analysis, last, steps)

            iterations(dve, body)


def kernel(L0_attn_x, L0_attn_h_filter, L0_attn_g_filter, L0_attn_h_synth, L0_attn_g_synth,
           L0_attn_norm_gamma, L0_attn_norm_beta, L0_ffn_w_gate, L0_ffn_w_up, L0_ffn_w_down):
    import numpy as np
    import concourse.bacc as bacc
    from concourse.bass_utils import run_bass_kernel_spmd

    x = np.ascontiguousarray(L0_attn_x)
    x_chan = np.zeros((P, BATCHES, NC, SEQ + 6 + TOK), x.dtype)
    x_chan[:, :, :, 3:3 + SEQ] = x.reshape(BATCHES, SEQ, NC, P).transpose(3, 0, 2, 1)
    taps = np.stack([np.asarray(f).reshape(4, NC, P) for f in
                     (L0_attn_h_filter, L0_attn_g_filter, L0_attn_h_synth, L0_attn_g_synth)])
    taps = np.ascontiguousarray(taps.transpose(3, 2, 0, 1).reshape(P, NC, 16))
    gamma = np.ascontiguousarray(np.broadcast_to(np.asarray(L0_attn_norm_gamma), (P, C)))
    beta = np.ascontiguousarray(np.broadcast_to(np.asarray(L0_attn_norm_beta), (P, C)))
    wg = np.asarray(L0_ffn_w_gate).reshape(HID, NC, P).transpose(2, 1, 0).reshape(P, NC * HID)
    wu = np.asarray(L0_ffn_w_up).reshape(HID, NC, P).transpose(2, 1, 0).reshape(P, NC * HID)
    wd = np.asarray(L0_ffn_w_down).reshape(C, NH, P).transpose(2, 1, 0).reshape(P, NH * C)
    weights = np.ascontiguousarray(np.concatenate([wg, wu, wd], axis=1))
    edge = np.ones((P, ITERS, 2), np.float32)
    edge[:, 0::PER_BATCH, 0] = 0.0
    edge[:, PER_BATCH - 1::PER_BATCH, 1] = 0.0
    edge = edge.reshape(P, 2 * ITERS)
    identity = np.eye(P, dtype=np.float32)
    block_mask = np.kron(np.eye(P // HEAD, dtype=np.float32), np.ones((HEAD, HEAD), np.float32))

    nc = bacc.Bacc("TRN2", target_bir_lowering=False, num_devices=1)
    arrays, args = {}, []
    for name, a in (("x_tok", x), ("x_chan", x_chan), ("taps", taps), ("gamma", gamma), ("beta", beta),
                    ("edge", edge), ("weights", weights), ("identity", identity), ("block_mask", block_mask)):
        arrays[name] = a
        args.append(nc.dram_tensor(name, a.shape, mybir.dt.from_np(a.dtype), kind="ExternalInput").ap())
    out = nc.dram_tensor("out", (BATCHES, SEQ, C), F32, kind="ExternalOutput").ap()
    mixer_ffn(nc, *args, out)
    result = run_bass_kernel_spmd(nc, [arrays], core_ids=[0])
    return result.results[0]["out"]
```

```python
from contextlib import ExitStack

import concourse.bass as bass
from concourse import mybir

P = 128
BATCHES, SEQ, C = 2, 4096, 512
HID = 1536
NC = C // P
NH = HID // P
TOK = 1024
PER_BATCH = SEQ // TOK
ITERS = BATCHES * PER_BATCH
BLK = 512
SUBS = TOK // P
DSUB = BLK // P
M1 = TOK // 2
M2 = TOK // 4
XW = TOK + 6
LW = M1 + 2
QW = M2 + 3
HEAD = 32
LN_EPS = 1e-5
ATTN_EPS = 1e-6
X1_SCALE = 2048.0
H_SCALE = 0.125
WSCALE = 1.0 / 127.0
PIECES = 12
PW = HID

F32 = mybir.dt.float32
F16 = mybir.dt.float16
I32 = mybir.dt.int32
ALU = mybir.AluOpType
ACT = mybir.ActivationFunctionType

H0, G0, S0, T0 = 0, 4, 8, 12
S12, S01, S23, T12, T01, T23 = 16, 17, 18, 19, 20, 21
NCOEF = 22

NEXT, NOW, ANA = "next iteration", "this iteration", "analysis"
BESIDE = {
    (0, 0): [(NOW, "norm2", 4), (NOW, "normq", 4), (NOW, "norm1", 6)],
    (0, 1): [(NOW, "normx", 4), (NOW, "norm2", 5), (NOW, "normq", 5), (NOW, "norm1", 7),
             (ANA, "low1", 0)],
    (0, 2): [(NOW, "norm3", 4), (NOW, "normx", 5), (NOW, "norm2", 6), (NOW, "normq", 6)],
    (0, 3): [(NOW, "norm3", 5), (NOW, "normx", 6), (NOW, "norm2", 7), (NOW, "normq", 7),
             (ANA, "low1", 1)],
    (0, 4): [(NOW, "norm3", 6), (NOW, "normx", 7), (NEXT, "high1", 0)],
    (0, 5): [(NOW, "norm3", 7)],
    (0, 6): [(NEXT, "dens", 0)],
    (0, 7): [(NEXT, "high1", 1)],
    (0, 8): [(NEXT, "attend", 0), (NEXT, "synth2", 0)],
    (0, 9): [(NEXT, "synth1a", 0)],
    (0, 11): [(NEXT, "synth1b", 0)],
    (0, 12): [(NEXT, "attend", 1), (NEXT, "synth2", 1)],
    (0, 13): [(NEXT, "synth1a", 1)],
    (0, 14): [(NEXT, "synth1b", 1)],
    (0, 15): [(NEXT, "attend", 2), (NEXT, "synth2", 2)],
    (1, 0): [(NEXT, "synth1a", 2)],
    (1, 1): [(NEXT, "synth1b", 2)],
    (1, 2): [(NEXT, "attend", 3), (NEXT, "synth2", 3)],
    (1, 3): [(NEXT, "synth1a", 3)],
    (1, 5): [(NEXT, "synth1b", 3), (ANA, "band2", 0)],
    (1, 6): [(ANA, "band2", 1)],
    (1, 7): [(NEXT, "norm1", 0), (ANA, "band2", 2)],
    (1, 8): [(NEXT, "norm2", 0), (NEXT, "normq", 0), (NEXT, "norm1", 1), (ANA, "band2", 3), (ANA, "exp", 0)],
    (1, 9): [(NEXT, "normx", 0), (NEXT, "norm2", 1), (NEXT, "normq", 1), (NEXT, "norm1", 2)],
    (1, 10): [(NEXT, "norm3", 0), (NEXT, "normx", 1), (NEXT, "norm2", 2), (NEXT, "normq", 2),
              (NEXT, "norm1", 3), (ANA, "keys", 0)],
    (1, 11): [(NEXT, "norm3", 1), (NEXT, "normx", 2), (NEXT, "norm2", 3), (NEXT, "normq", 3)],
    (1, 12): [(NEXT, "norm3", 2), (NEXT, "normx", 3), (ANA, "turn", 0), (ANA, "turn", 1), (ANA, "turn", 2),
              (ANA, "turn", 3)],
    (1, 13): [(ANA, "kv", 0), (NEXT, "norm3", 3), (ANA, "blocks", 0)],
    (1, 14): [(NEXT, "norm1", 4)],
    (1, 15): [(NEXT, "norm1", 5)],
}
THEN, THIS = "former analysis", "this analysis"
OPEN = [(THEN, "keys", 0), (THIS, "low1", 0), (THIS, "weights", 0), (THIS, "conv1", 2), (THIS, "out1", 2),
        (THEN, "turn", 0), (THEN, "turn", 1), (THIS, "conv1", 3), (THIS, "out1", 3), (THEN, "turn", 2),
        (THEN, "turn", 3), (THIS, "band2", 0), (THIS, "band2", 1), (THIS, "conv2", 2), (THIS, "cast", 0),
        (THEN, "kv", 0), (THIS, "conv2", 3), (THEN, "kv_add", 0), (THIS, "out2", 2), (THIS, "out2", 3),
        (THIS, "exp", 0)]
CLOSE = [(name, n) for which, name, n in OPEN if which is THEN]
FIRST_MIX = [("high1", 0), ("dens", 0), ("high1", 1), ("attend", 0)]
for _c in range(NC):
    FIRST_MIX += [("synth2", _c)] + ([("attend", _c + 1)] if _c + 1 < NC else []) + \
                 [("synth1a", _c), ("synth1b", _c)]
FIRST_NORM = []
for _s in range(7):
    FIRST_NORM += ([("norm3", _s - 3)] if 0 <= _s - 3 < 4 else []) + ([("normx", _s - 2)] if 0 <= _s - 2 < 4 else []) + \
                  ([("norm2", _s - 1), ("normq", _s - 1)] if 0 <= _s - 1 < 4 else []) + \
                  ([("norm1", _s)] if _s < 6 else [])

N_HIGH1, N_LOW1, N_BAND2, N_SYN2, N_SYN1, N_KEYS, N_BLOCKS = 8, 8, 7, 9, 10, 5, 5
AHEAD = PER_BATCH + 1
HEADS = C // HEAD


def mixer_ffn(nc, x_tok, x_chan, taps, gamma, beta, edge, weights, identity, block_mask, head_mask, head_spread,
              out):
    q_dram = nc.dram_tensor("q_scratch", [P, BATCHES, NC, SEQ // 4 + 3], F32, kind="Internal").ap()
    h2_dram = nc.dram_tensor("h2_scratch", [P, BATCHES, NC, SEQ // 4 + 3], F32, kind="Internal").ap()

    with ExitStack() as ctx:
        def sb(name, shape, dt=F32):
            return ctx.enter_context(nc.sbuf_tensor(name, shape, dt))

        def sem(name):
            return ctx.enter_context(nc.semaphore(name))

        w16 = sb("w16", [P, PIECES * PW], F16)
        coef = sb("coef", [P, NC, NCOEF])
        gamma_b = sb("gamma_b", [P, C])
        beta_b = sb("beta_b", [P, C])
        edge_sb = sb("edge_sb", [P, 2 * ITERS])
        ident = sb("ident", [P, P])
        mask = sb("mask", [P, P])
        zeros = sb("zeros", [P, 16])
        minus_half = sb("minus_half", [P, 1])
        eps1 = sb("eps1", [P, 1])
        xa = sb("xa", [P, NC, XW])
        l1 = sb("l1", [P, NC, LW])
        l2 = sb("l2", [P, NC, M2])
        h2 = sb("h2", [P, NC, M2])
        keys = sb("keys", [P, NC, M2])
        kv_sum = sb("kv_sum", [P, NC * P])
        z_part = sb("z_part", [P, NC])
        z_sum = sb("z_sum", [P, NC])
        kv_blocks = sb("kv_blocks", [P, NC, P])
        z_heads = sb("z_heads", [P, NC, HEADS])
        head_of = sb("head_of", [P, NC, HEADS])
        spread = sb("spread", [HEADS, NC, P])
        den = sb("den", [HEADS, QW])
        xb = sb("xb", [P, NC, XW])
        q_in = sb("q_in", [P, NC, QW])
        h2_in = sb("h2_in", [P, NC, QW])
        h1_mem = sb("h1_mem", [P, NC * LW])
        h1 = h1_mem[:, :].rearrange("p (c n) -> p c n", c=NC)
        kvt = h1_mem[:, 0:NC * 4 * P].rearrange("p (c n) -> p c n", c=NC)
        low = sb("low", [P, 2, LW])
        att = sb("att", [P, 2, QW])
        xt = sb("xt", [P, 4, C])
        s_chan = sb("s_chan", [P, NC, TOK])
        x1 = sb("x1", [P, SUBS, C])
        junk = sb("junk", [P, C], F16)
        st1 = sb("st1", [P, SUBS, 6])
        mv1 = sb("mv1", [P, SUBS, 2])
        rs1 = sb("rs1", [P, SUBS, 2])
        rs2 = sb("rs2", [P, SUBS, 6])
        x1_hi = sb("x1_hi", [P, 2, NC, BLK], F16)
        x1_lo = sb("x1_lo", [P, 2, NC, BLK], F16)
        hid = sb("hid", [P, 2 * NH * BLK], F16)
        h_hi = hid[:, 0:NH * BLK].rearrange("p (k n) -> p k n", k=NH)
        h_lo = hid[:, NH * BLK:2 * NH * BLK].rearrange("p (k n) -> p k n", k=NH)
        stage = hid[:, :].bitcast(I32)
        gate_s = sb("gate_s", [P, 2, BLK])
        h_f = sb("h_f", [P, 2, BLK])
        z = sb("z", [P, DSUB, C])
        rs3 = sb("rs3", [P, DSUB, 6])
        minus_part = sb("minus_part", [P, 1])

        ps_gu = [[ctx.enter_context(nc.psum_tensor(f"ps_{n}{k}", [P, BLK], F32)) for n in ("gate", "up")]
                 for k in range(2)]
        ps_d = [ctx.enter_context(nc.psum_tensor(f"ps_down{k}", [P, C], F32)) for k in range(2)]
        ps_x = ctx.enter_context(nc.psum_tensor("ps_x", [P, 512], F32))
        ps_y = ctx.enter_context(nc.psum_tensor("ps_y", [P, 512], F32))

        ld_const, zero_pads = sem("ld_const"), sem("zero_pads")
        ld_w = [sem(f"ld_w{n}") for n in range(3)]
        ld_xa = [sem(f"ld_xa{c}") for c in range(NC)]
        ld_xb, ld_q, ld_h2 = sem("ld_xb"), sem("ld_q"), sem("ld_h2")
        ld_xt = [sem(f"ld_xt{n}") for n in range(4)]
        st_q, st_h2 = sem("st_q"), sem("st_h2")
        st_out = [sem(f"st_out{t}") for t in range(DSUB)]
        set_dve, set_pool, coef_ready, w_cast = sem("set_dve"), sem("set_pool"), sem("coef_ready"), sem("w_cast")
        sums_zero = sem("sums_zero")
        l1_first, band2_first, low1_step, band2_step = (sem("l1_first"), sem("band2_first"), sem("low1_step"),
                                                        sem("band2_step"))
        exp_done, keys_step, turned, turn_out = sem("exp_done"), sem("keys_step"), sem("turned"), sem("turn_out")
        kv_ready, kv_added, blocks_step = sem("kv_ready"), sem("kv_added"), sem("blocks_step")
        diag_ready, conv1_ready, conv2_ready = sem("diag_ready"), sem("conv1_ready"), sem("conv2_ready")
        h1_first, low_first, high1_step = sem("h1_first"), sem("low_first"), sem("high1_step")
        den_ready, den_step, qk_ready, rden_out, att_done = (sem("den_ready"), sem("den_step"), sem("qk_ready"),
                                                             sem("rden_out"), sem("att_done"))
        syn2_step, syn1_step = sem("syn2_step"), sem("syn1_step")
        s_ready, s_stats, s_mv, s_centred = sem("s_ready"), sem("s_stats"), sem("s_mv"), sem("s_centred")
        var1_eps, rstd1, x_beta = sem("var1_eps"), sem("rstd1"), sem("x_beta")
        r_ready, nmean2, r_squares, var2, rstd2, shift2 = (sem("r_ready"), sem("nmean2"), sem("r_squares"),
                                                           sem("var2"), sem("rstd2"), sem("shift2"))
        x1_ready, x1_turned, x1_hi_ready, x1_lo_ready = (sem("x1_ready"), sem("x1_turned"), sem("x1_hi_ready"),
                                                         sem("x1_lo_ready"))
        gu_ready, silu_done, h_mul, hi_done, lo_done = (sem("gu_ready"), sem("silu_done"), sem("h_mul"),
                                                        sem("hi_done"), sem("lo_done"))
        d_ready, z_done, nmean3, z_squares = sem("d_ready"), sem("z_done"), sem("nmean3"), sem("z_squares")
        var3, rstd3, shift3, out_done = sem("var3"), sem("rstd3"), sem("shift3"), sem("out_done")

        def hold(eng, semaphore, value):
            eng.wait_ge(semaphore, value)
            eng.nop(nofuse=True)

        def before(steps):
            def run(names, index, batch):
                for name, n in names:
                    if name in steps:
                        steps[name](index, batch, n)
            return run

        def diag(n):
            return z[:, n // 4, (n % 4) * P:(n % 4 + 1) * P]

        def before_analyses(eng, steps):
            def analysis(a, batch=0):
                for which, name, n in OPEN:
                    if name not in steps:
                        continue
                    if which is THIS:
                        steps[name](a, batch, n)
                    elif not first(a):
                        steps[name](a - 1, 0, n)

            analysis(0)
            analysis(1)
            with eng.Fori(2, PER_BATCH) as a:
                analysis(a)
            analysis(PER_BATCH, 1)
            before(steps)(CLOSE, PER_BATCH, 1)

        def first(index):
            return isinstance(index, int) and index == 0

        def iterations(eng, body):
            with eng.Fori(0, 2) as i:
                body(i, 0, True, False)
            body(2, 0, True, True)
            body(3, 0, False, True)
            with eng.Fori(PER_BATCH, ITERS - 1) as i:
                body(i, 1, False, False)
            body(ITERS - 1, 1, False, True)

        def beside(b, k, i, batch, analysis, last, steps):
            for which, name, n in BESIDE.get((b, k), []):
                if name not in steps:
                    continue
                if which is NOW:
                    steps[name](i, batch, n)
                elif which is NEXT and not (last and batch == 1):
                    steps[name](i + 1, batch + (1 if last and not analysis else 0), n)
                elif which is ANA and analysis and (name != "blocks" or last):
                    steps[name](i + AHEAD, 1, n)

        block = ctx.enter_context(nc.Block())

        @block.sync
        def _(sp):
            def load_xa(a, c):
                sp.dma_start(xa[:, c, :], x_chan[:, bass.ds(a, 1), c, :]).then_inc(ld_xa[c], 16)

            def low1(a, batch, p):
                if isinstance(a, int) and a == ITERS - 1:
                    return
                hold(sp, low1_step, (2 * a + p) * N_LOW1 + 6)
                load_xa(a + 1, 2 * p)
                load_xa(a + 1, 2 * p + 1)

            def keys_store(a, batch, _):
                at = (a - PER_BATCH * batch) * M2 + 1
                hold(sp, band2_step, (a + 1) * NC * N_BAND2)
                sp.dma_start(h2_dram[:, batch, :, bass.ds(at, M2)], h2[:, :, :]).then_inc(st_h2, 16)
                hold(sp, keys_step, (a + 1) * N_KEYS)
                sp.dma_start(q_dram[:, batch, :, bass.ds(at, M2)], keys[:, :, :]).then_inc(st_q, 16)

            def load_xb(j):
                sp.dma_start(xb[:, :, :], x_chan[:, bass.ds(j, 1), :, :].rearrange("p a c n -> p (a c) n")
                             ).then_inc(ld_xb, 16)

            def load_bands(j, batch):
                at = (j - PER_BATCH * batch) * M2
                hold(sp, st_q, 16 * PER_BATCH * (batch + 1))
                hold(sp, st_h2, 16 * PER_BATCH * (batch + 1))
                sp.dma_start(q_in[:, :, :], q_dram[:, batch, :, bass.ds(at, QW)]).then_inc(ld_q, 16)
                sp.dma_start(h2_in[:, :, :], h2_dram[:, batch, :, bass.ds(at, QW)]).then_inc(ld_h2, 16)

            def load_xt(j, t):
                sp.dma_start(xt[:, t % 4, :], x_tok[bass.ds(j * TOK + t * P, P), :]).then_inc(ld_xt[t % 4], 16)

            def after_norm2(j, batch, t):
                if isinstance(j, int) and j == ITERS - 1 and t >= 4:
                    return
                hold(sp, r_ready, SUBS * j + t + 1)
                load_xt(j + (t + 4) // SUBS, (t + 4) % SUBS)

            def load_weights(a, batch, _):
                if isinstance(a, int) and a == PER_BATCH:
                    return
                for n in range(3):
                    if not first(a):
                        hold(sp, w_cast, 3 * a)
                    sp.dma_start(stage[:, n * PW:(n + 1) * PW], weights[:, bass.ds((a * 3 + n) * PW, PW)]
                                 ).then_inc(ld_w[n], 16)

            def out1(a, batch, c):
                if c == 3:
                    low1(a, batch, 1)

            def first_bands(a, batch, _):
                if isinstance(a, int) and a == PER_BATCH - 1:
                    hold(sp, zero_pads, 64)
                    load_bands(0, 0)
                    for t in range(4):
                        load_xt(0, t)

            steps = {"low1": low1, "keys": keys_store, "norm2": after_norm2}
            run = before(steps)

            for c in range(NC):
                load_xa(0, c)
            for dst, src in ((coef[:, :, 0:16], taps), (edge_sb[:, :], edge), (ident[:, :], identity),
                             (mask[:, :], block_mask), (head_of[:, :, :], head_mask),
                             (spread[:, :, :], head_spread), (gamma_b[:, :], gamma), (beta_b[:, :], beta)):
                sp.dma_start(dst, src).then_inc(ld_const, 16)
            hold(sp, set_dve, 1)
            for dram in (q_dram, h2_dram):
                for at, width in ((0, 1), (SEQ // 4 + 1, 2)):
                    sp.dma_start(dram[:, :, :, at:at + width], zeros[:, 0:8 * width].rearrange(
                        "p (b c w) -> p b c w", b=BATCHES, c=NC), allow_slow_non_contiguous=True
                        ).then_inc(zero_pads, 16)
            load_xb(0)
            before_analyses(sp, {**steps, "out1": out1, "weights": load_weights, "kv": first_bands})
            run(FIRST_NORM, 0, 0)

            def body(i, batch, analysis, last):
                more = not (last and batch == 1)
                for b in range(2):
                    for k in range(NH + DSUB):
                        if (b, k) == (0, 0) and more:
                            hold(sp, syn1_step, N_SYN1 * NC * (i + 1))
                            load_xb(i + 1)
                            load_bands(i + 1, batch + (1 if last and not analysis else 0))
                        beside(b, k, i, batch, analysis, last, steps)
                        if k >= NH:
                            t = k - NH
                            B = 2 * i + b
                            hold(sp, out_done, DSUB * B + t + 1)
                            sp.dma_start(out[bass.ds(B * BLK + t * P, P), :], z[:, t, :]).then_inc(st_out[t], 16)

            iterations(sp, body)
            for t in range(DSUB):
                hold(sp, st_out[t], 16 * (2 * ITERS + 1))

        @block.tensor
        def _(pe):
            def turn(a, batch, c):
                bank = (ps_x, ps_y)[c % 2]
                beside_mix = batch == 1 and not (isinstance(a, int) and a == PER_BATCH)
                if c == 0:
                    pe.wait_ge(keys_step, (a + 1) * N_KEYS - 1)
                    if not first(a):
                        pe.wait_ge(kv_added, a)
                    if beside_mix:
                        pe.wait_ge(s_centred, SUBS * (a - PER_BATCH) + 4)
                if c == 1 and beside_mix:
                    pe.wait_ge(x1_lo_ready, SUBS * (a - PER_BATCH) + 3)
                if c >= 2:
                    pe.wait_ge(turn_out, NC * a + c - 1)
                for n, src in enumerate((keys[:, c, 0:P], keys[:, c, P:2 * P], l2[:, c, 0:P], l2[:, c, P:2 * P])):
                    mm = pe.transpose(bank[:, n * P:(n + 1) * P], src, ident[:, :])
                mm.then_inc(turned, 1)

            def kv(a, batch, _):
                pe.wait_ge(turn_out, NC * (a + 1))
                for c in range(NC):
                    for n in range(2):
                        mm = pe.matmul(ps_x[:, c * P:(c + 1) * P], kvt[:, c, n * P:(n + 1) * P],
                                       kvt[:, c, (2 + n) * P:(3 + n) * P], start=(n == 0), stop=(n == 1))
                mm.then_inc(kv_ready, 1)

            def dens(j, batch, _):
                pe.wait_ge(ld_q, 16 * (j + 1))
                pe.wait_ge(blocks_step, N_BLOCKS * (batch + 1))
                if first(j):
                    pe.wait_ge(turn_out, NC * AHEAD)
                else:
                    pe.wait_ge(x1_lo_ready, SUBS * j)
                for c in range(NC):
                    mm = pe.matmul(ps_y[0:HEADS, 0:QW], z_heads[:, c, :], q_in[:, c, :], start=(c == 0),
                                   stop=(c == NC - 1))
                mm.then_inc(den_ready, 1)

            def attend(j, batch, c):
                if c == 0:
                    pe.wait_ge(den_step, 2 * (j + 1))
                    if first(j):
                        pe.wait_ge(kv_added, AHEAD)
                    else:
                        pe.wait_ge(s_centred, SUBS * j)
                else:
                    pe.wait_ge(att_done, NC * j + c)
                pe.matmul(ps_y[:, 0:QW], spread[:, c, :], den[:, :], start=True, stop=True)
                pe.matmul(ps_x[:, 0:QW], kv_blocks[:, c, :], q_in[:, c, :], start=True, stop=True
                          ).then_inc(qk_ready, 1)

            def norm1(j, batch, t):
                if t == 0:
                    pe.wait_ge(syn1_step, N_SYN1 * NC * (j + 1))
                    pe.wait_ge(att_done, NC * (j + 1))
                else:
                    pe.wait_ge(s_centred, SUBS * j + t)
                if t == 4 and batch == 0:
                    pe.wait_ge(kv_added, j + AHEAD)
                for c in range(NC):
                    mm = pe.transpose(ps_x[:, c * P:(c + 1) * P], s_chan[:, c, t * P:(t + 1) * P], ident[:, :])
                mm.then_inc(s_ready, 1)

            def norm3(j, batch, t):
                s = SUBS * j + t
                pe.wait_ge(x1_ready, s + 1)
                if t == 0:
                    pe.wait_ge(att_done, NC * (j + 1))
                else:
                    pe.wait_ge(x1_lo_ready, s)
                if t == 3 and batch == 0:
                    pe.wait_ge(turn_out, NC * (j + AHEAD))
                for c in range(NC):
                    mm = pe.transpose(ps_y[:, c * P:(c + 1) * P], x1[:, t, c * P:(c + 1) * P], ident[:, :])
                mm.then_inc(x1_turned, 1)

            steps = {"turn": turn, "kv": kv, "dens": dens, "attend": attend, "norm1": norm1, "norm3": norm3}

            def gate_up(B, b, k):
                if k == 0:
                    pe.wait_ge(x1_hi_ready, DSUB * (B + 1))
                    pe.wait_ge(x1_lo_ready, DSUB * (B + 1))
                pe.wait_ge(h_mul, NH * B + k + 1)
                for g in range(2):
                    for c in range(NC):
                        w = w16[:, (g * NC + c) * PW + k * P:(g * NC + c) * PW + (k + 1) * P]
                        pe.matmul(ps_gu[k % 2][g][:, :], w, x1_hi[:, b, c, :], start=(c == 0), stop=False)
                        mm = pe.matmul(ps_gu[k % 2][g][:, :], w, x1_lo[:, b, c, :], start=False, stop=(c == NC - 1))
                mm.then_inc(gu_ready, 1)

            def down(B, t):
                pe.wait_ge(z_done, DSUB * B + t + 1)
                for k in range(NH):
                    if t == 0 and k >= NH - 3:
                        pe.wait_ge(hi_done, NH * B + k + 1)
                        pe.wait_ge(lo_done, NH * B + k + 1)
                    elif t == 0 and k == 0:
                        pe.wait_ge(hi_done, NH * B + NH - 3)
                        pe.wait_ge(lo_done, NH * B + NH - 3)
                    w = w16[:, 2 * NC * PW + k * C:2 * NC * PW + (k + 1) * C]
                    pe.matmul(ps_d[t % 2][:, :], h_hi[:, k, t * P:(t + 1) * P], w, start=(k == 0), stop=False)
                    mm = pe.matmul(ps_d[t % 2][:, :], h_lo[:, k, t * P:(t + 1) * P], w, start=False,
                                   stop=(k == NH - 1))
                mm.then_inc(d_ready, 1)

            def body(i, batch, analysis, last):
                for b in range(2):
                    for k in range(NH):
                        gate_up(2 * i + b, b, k)
                        beside(b, k, i, batch, analysis, last, steps)
                    for t in range(DSUB):
                        beside(b, NH + t, i, batch, analysis, last, steps)
                        down(2 * i + b, t)

            def conv1(a, batch, c):
                half = LW // 2
                pe.wait_ge(ld_xa[c], 16 * (a + 1))
                for n in range(2):
                    for k in range(4):
                        at = 2 * n * half + k
                        mm = pe.matmul(ps_gu[c - 2][n][:, 0:half], diag(8 * (c - 2) + k),
                                       xa[:, c, at:at + 2 * half - 1:2], start=(k == 0), stop=(k == 3))
                mm.then_inc(conv1_ready, 1)

            def conv2(a, batch, c):
                pe.wait_ge(low1_step, (2 * a + 2) * N_LOW1)
                for g in range(2):
                    for k in range(4):
                        mm = pe.matmul(ps_d[c - 2][:, g * M2:(g + 1) * M2], diag(8 * (c - 2) + 4 * g + k),
                                       l1[:, c, k:k + 2 * M2 - 1:2], start=(k == 0), stop=(k == 3))
                mm.then_inc(conv2_ready, 1)

            pe.wait_ge(ld_const, 128)
            pe.wait_ge(diag_ready, 16)
            before_analyses(pe, {**steps, "conv1": conv1, "conv2": conv2})
            run = before(steps)
            run(FIRST_MIX + FIRST_NORM, 0, 0)
            pe.wait_ge(w_cast, PIECES)
            iterations(pe, body)

        @block.scalar
        def _(act):
            def first_tap(dst, src, c, tap, done):
                nc.scalar.activation(dst, src, ACT.Copy, scale=coef[:, c, tap:tap + 1]).then_inc(done, 1)

            def low1(a, batch, p):
                for c in (2 * p, 2 * p + 1):
                    act.wait_ge(ld_xa[c], 16 * (a + 1))
                    if c == 0 and not first(a):
                        act.wait_ge(band2_step, NC * N_BAND2 * a)
                    first_tap(l1[:, c, :], xa[:, c, 0:2 * LW - 1:2], c, H0, l1_first)

            def band2(a, batch, c):
                act.wait_ge(low1_step, (2 * a + c // 2 + 1) * N_LOW1)
                if c == 0 and not first(a):
                    act.wait_ge(keys_step, N_KEYS * a)
                    act.wait_ge(turned, NC * a)
                    act.wait_ge(st_h2, 16 * a)
                first_tap(l2[:, c, :], l1[:, c, 0:2 * M2 - 1:2], c, H0, band2_first)
                first_tap(h2[:, c, :], l1[:, c, 0:2 * M2 - 1:2], c, G0, band2_first)

            def exp(a, batch, _):
                act.wait_ge(band2_step, NC * N_BAND2 * (a + 1))
                nc.scalar.activation(keys[:, :, :], keys[:, :, :], ACT.Exp).then_inc(exp_done, 1)

            def turn(a, batch, c):
                act.wait_ge(turned, NC * a + c + 1)
                if c == 0:
                    if batch == 1 and not (isinstance(a, int) and a == PER_BATCH):
                        act.wait_ge(syn1_step, N_SYN1 * NC * (a - PER_BATCH + 1))
                    if not first(a):
                        act.wait_ge(kv_ready, a)
                nc.scalar.activation(kvt[:, c, :], (ps_x, ps_y)[c % 2][:, :], ACT.Copy).then_inc(turn_out, 1)

            def high1(j, batch, p):
                if p == 0:
                    act.wait_ge(ld_xb, 16 * (j + 1))
                    if not first(j):
                        act.wait_ge(syn1_step, N_SYN1 * NC * j)
                    if first(j):
                        act.wait_ge(kv_ready, AHEAD)
                    elif batch == 0 or isinstance(j, int):
                        act.wait_ge(kv_ready, j + PER_BATCH)
                for c in (2 * p, 2 * p + 1):
                    first_tap(h1[:, c, :], xb[:, c, 0:2 * LW - 1:2], c, G0, h1_first)

            def synth2(j, batch, c):
                if c == 0:
                    act.wait_ge(ld_h2, 16 * (j + 1))
                if not (isinstance(j, int) and NC * j + c < 2):
                    act.wait_ge(syn1_step, N_SYN1 * (NC * j + c - 1))
                u = M2 + 1
                first_tap(low[:, c % 2, 0:2 * u - 1:2], h2_in[:, c, 0:u], c, T01, low_first)
                first_tap(low[:, c % 2, 1:2 * u:2], h2_in[:, c, 0:u], c, T0, low_first)

            def attend(j, batch, c):
                act.wait_ge(qk_ready, NC * j + c + 1)
                if not (isinstance(j, int) and NC * j + c < 2):
                    act.wait_ge(syn2_step, N_SYN2 * (NC * j + c - 1))
                nc.scalar.activation(att[:, c % 2, :], ps_y[:, 0:QW], ACT.Copy).then_inc(rden_out, 1)

            def normq(j, batch, t):
                act.wait_ge(nmean2, SUBS * j + t + 1)
                nc.scalar.activation(junk[:, :], x1[:, t, :], ACT.Square, bias=rs2[:, t, 1:2],
                                     accum_out=rs2[:, t, 2:3]).then_inc(r_squares, 1)

            def normx(j, batch, t):
                act.wait_ge(shift2, SUBS * j + t + 1)
                act.wait_ge(r_squares, SUBS * j + t + 1)
                nc.scalar.activation(x1[:, t, :], x1[:, t, :], ACT.Identity, bias=rs2[:, t, 5:6],
                                     scale=rs2[:, t, 4:5]).then_inc(x1_ready, 1)

            def norm3(j, batch, t):
                act.wait_ge(x1_turned, SUBS * j + t + 1)
                nc.scalar.activation(x1_hi[:, t // DSUB, :, (t % DSUB) * P:(t % DSUB + 1) * P],
                                     ps_y[:, :].rearrange("p (c n) -> p c n", c=NC), ACT.Copy
                                     ).then_inc(x1_hi_ready, 1)

            early = {"low1": low1, "band2": band2, "high1": high1, "attend": attend, "synth2": synth2,
                     "norm3": norm3}
            late = {"exp": exp, "turn": turn, "normq": normq, "normx": normx}

            def out1(a, batch, c):
                half = LW // 2
                act.wait_ge(conv1_ready, 2 * a + c - 1)
                nc.scalar.activation(l1[:, c, 0:half], ps_gu[c - 2][0][:, 0:half], ACT.Copy)
                nc.scalar.activation(l1[:, c, half:LW], ps_gu[c - 2][1][:, 0:half], ACT.Copy
                                     ).then_inc(l1_first, 1)

            def out2(a, batch, c):
                act.wait_ge(conv2_ready, 2 * a + c - 1)
                for g, band in enumerate((l2, h2)):
                    nc.scalar.activation(band[:, c, :], ps_d[c - 2][:, g * M2:(g + 1) * M2], ACT.Copy
                                         ).then_inc(band2_first, 1)

            def cast_weights(a, batch, _):
                if isinstance(a, int) and a == PER_BATCH:
                    return
                for n in range(3):
                    act.wait_ge(ld_w[n], 16 * (a + 1))
                    nc.scalar.activation(w16[:, bass.ds((a * 3 + n) * PW, PW)], stage[:, n * PW:(n + 1) * PW],
                                         ACT.Copy).then_inc(w_cast, 1)

            act.wait_ge(coef_ready, 6)
            before_analyses(act, {**early, **late, "out1": out1, "out2": out2, "cast": cast_weights})
            run = before({**early, **late})
            run(FIRST_MIX + FIRST_NORM, 0, 0)

            def normalise(B, t):
                act.wait_ge(shift3, DSUB * B + t + 1)
                nc.scalar.activation(z[:, t, :], z[:, t, :], ACT.Identity, bias=rs3[:, t, 5:6],
                                     scale=rs3[:, t, 4:5]).then_inc(out_done, 1)

            def body(i, batch, analysis, last):
                for b in range(2):
                    B = 2 * i + b
                    for k in range(NH):
                        act.wait_ge(gu_ready, NH * B + k + 1)
                        nc.scalar.activation(gate_s[:, k % 2, :], ps_gu[k % 2][0][:, :], ACT.Silu,
                                             scale=WSCALE / X1_SCALE).then_inc(silu_done, 1)
                        beside(b, k, i, batch, analysis, last, early)
                        act.wait_ge(h_mul, NH * B + k + 3)
                        nc.scalar.activation(h_hi[:, k, :], h_f[:, k % 2, :], ACT.Copy).then_inc(hi_done, 1)
                        beside(b, k, i, batch, analysis, last, late)
                    for t in range(DSUB):
                        beside(b, NH + t, i, batch, analysis, last, early)
                        if t > 0:
                            normalise(B, t - 1)
                        beside(b, NH + t, i, batch, analysis, last, late)
                        act.wait_ge(nmean3, DSUB * B + t + 1)
                        nc.scalar.activation(junk[:, :], z[:, t, :], ACT.Square, bias=rs3[:, t, 1:2],
                                             accum_out=rs3[:, t, 2:3]).then_inc(z_squares, 1)
                    normalise(B, DSUB - 1)

            iterations(act, body)

        @block.gpsimd
        def _(pool):
            nc.gpsimd.memset(minus_half[:], -0.5).then_inc(set_pool, 1)
            nc.gpsimd.memset(eps1[:], LN_EPS).then_inc(set_pool, 1)
            nc.gpsimd.memset(minus_part[:], -1.0 / C).then_inc(set_pool, 1)
            pool.wait_ge(set_pool, 3)
            pool.wait_ge(ld_const, 128)
            for n in range(16):
                c = 2 + n // 8
                nc.gpsimd.tensor_tensor(diag(n), ident[:, :], coef[:, c, n % 8:n % 8 + 1].to_broadcast([P, P]), ALU.mult
                                        ).then_inc(diag_ready, 1)

            def norm1(j, batch, t):
                s = SUBS * j + t
                pool.wait_ge(s_mv, s + 1)
                nc.gpsimd.tensor_tensor(rs1[:, t, 0:1], mv1[:, t, 1:2], eps1[:, :], ALU.add).then_inc(var1_eps, 1)
                pool.wait_ge(var1_eps, s + 1)
                nc.gpsimd.tensor_tensor(rs1[:, t, 1:2], rs1[:, t, 0:1], minus_half[:, :], ALU.pow
                                        ).then_inc(rstd1, 1)

            def xbeta(j, batch, t):
                pool.wait_ge(ld_xt[t % 4], 16 * (2 * j + t // 4 + 1))
                nc.gpsimd.tensor_tensor(xt[:, t % 4, :], xt[:, t % 4, :], beta_b[:, :], ALU.add
                                        ).then_inc(x_beta, 1)

            def norm1_and_x(j, batch, t):
                xbeta(j, batch, t)
                norm1(j, batch, t)

            def norm2(j, batch, t):
                pool.wait_ge(r_ready, SUBS * j + t + 1)
                nc.gpsimd.tensor_tensor(rs2[:, t, 1:2], rs2[:, t, 0:1], minus_part[:, :], ALU.mult
                                        ).then_inc(nmean2, 1)

            def scale_and_shift(rs, n, squares, eps, shrink, var, rstd, shift):
                hold(pool, squares, n)
                nc.gpsimd.tensor_scalar(rs[:, 3:4], rs[:, 2:3], shrink / C, eps * shrink, ALU.mult, ALU.add
                                        ).then_inc(var, 1)
                pool.wait_ge(var, n)
                nc.gpsimd.tensor_tensor(rs[:, 4:5], rs[:, 3:4], minus_half[:, :], ALU.pow).then_inc(rstd, 1)
                pool.wait_ge(rstd, n)
                nc.gpsimd.tensor_tensor(rs[:, 5:6], rs[:, 1:2], rs[:, 4:5], ALU.mult).then_inc(shift, 1)

            def normq(j, batch, t):
                scale_and_shift(rs2[:, t, :], SUBS * j + t + 1, r_squares, LN_EPS, X1_SCALE ** -2,
                                var2, rstd2, shift2)

            steps = {"norm1": norm1_and_x, "norm2": norm2, "normq": normq}
            before(steps)(FIRST_NORM, 0, 0)

            def body(i, batch, analysis, last):
                for b in range(2):
                    for k in range(NH + DSUB):
                        beside(b, k, i, batch, analysis, last, steps)
                        if k >= NH:
                            t = k - NH
                            n = DSUB * (2 * i + b) + t + 1
                            pool.wait_ge(z_done, n + 2)
                            nc.gpsimd.tensor_tensor(rs3[:, t, 1:2], rs3[:, t, 0:1], minus_part[:, :], ALU.mult
                                                    ).then_inc(nmean3, 1)
                            scale_and_shift(rs3[:, t, :], n, z_squares, LN_EPS * X1_SCALE ** 2, 1.0,
                                            var3, rstd3, shift3)

            iterations(pool, body)

        @block.vector
        def _(dve):
            V = nc.vector
            V.memset(zeros[:], 0.0).then_inc(set_dve, 1)
            V.memset(kv_sum[:], 0.0).then_inc(h_mul, 2)
            V.memset(z_sum[:], 0.0).then_inc(z_done, 2)
            dve.wait_ge(ld_const, 128)
            for dst, a, b in ((S12, S0 + 1, S0 + 2), (S01, S0, S0 + 1), (S23, S0 + 2, S0 + 3),
                              (T12, T0 + 1, T0 + 2), (T01, T0, T0 + 1), (T23, T0 + 2, T0 + 3)):
                V.tensor_tensor(coef[:, :, dst:dst + 1], coef[:, :, a:a + 1], coef[:, :, b:b + 1], ALU.add
                                ).then_inc(coef_ready, 1)
            dve.wait_ge(coef_ready, 6)
            for t in range(DSUB):
                V.memset(h_f[:, 0, t:t + 1], 0.0).then_inc(st_out[t], 16)

            def tap(acc, src, c, n, add=None):
                return V.scalar_tensor_tensor(out=acc, in0=src, scalar=coef[:, c, n:n + 1],
                                              in1=acc if add is None else add, op0=ALU.mult, op1=ALU.add)

            def edges(band, j):
                return V.tensor_tensor(band[:, 0:LW:LW - 1], band[:, 0:LW:LW - 1],
                                       edge_sb[:, bass.ds(2 * j, 2)], ALU.mult)

            def pair_taps(dst, src, p, g, j, first_done, step, base):
                for k in range(1, 4):
                    for u in range(2):
                        c = 2 * p + u
                        if k == 1:
                            dve.wait_ge(first_done, NC * j + c + 1)
                        else:
                            dve.wait_ge(step, base + 2 * (k - 2) + u + 1)
                        tap(dst[:, c, :], src[:, c, k:k + 2 * LW - 1:2], c, g + k).then_inc(step, 1)
                for u in range(2):
                    dve.wait_ge(step, base + 5 + u)
                    edges(dst[:, 2 * p + u, :], j).then_inc(step, 1)

            def low1(a, batch, p):
                pair_taps(l1, xa, p, H0, a, l1_first, low1_step, (2 * a + p) * N_LOW1)

            def band2(a, batch, c):
                n = (NC * a + c) * N_BAND2
                dve.wait_ge(low1_step, (2 * a + c // 2 + 1) * N_LOW1)
                dve.wait_ge(band2_first, 2 * (NC * a + c + 1))
                for k in range(1, 4):
                    for which, (band, g) in enumerate(((l2, H0), (h2, G0))):
                        if k > 1:
                            dve.wait_ge(band2_step, n + 2 * (k - 1) + which - 1)
                        tap(band[:, c, :], l1[:, c, k:k + 2 * M2 - 1:2], c, g + k).then_inc(band2_step, 1)
                dve.wait_ge(band2_step, n + 5)
                if c == 0 and not first(a):
                    dve.wait_ge(turned, NC * a)
                    dve.wait_ge(st_q, 16 * a)
                V.tensor_scalar(keys[:, c, :], l2[:, c, :], 0.0, None, ALU.min).then_inc(band2_step, 1)

            def keys_sum(a, batch, _):
                dve.wait_ge(exp_done, a + 1)
                for c in range(NC):
                    V.scalar_tensor_tensor(out=keys[:, c, :], in0=l2[:, c, :], scalar=0.0, in1=keys[:, c, :],
                                           op0=ALU.max, op1=ALU.add, accum_out=z_part[:, c:c + 1]
                                           ).then_inc(keys_step, 1)
                dve.wait_ge(keys_step, N_KEYS * a + NC)
                V.tensor_tensor(z_sum[:, :], z_sum[:, :], z_part[:, :], ALU.add).then_inc(keys_step, 1)

            def kv(a, batch, _):
                dve.wait_ge(kv_ready, a + 1)
                V.tensor_tensor(kv_sum[:, :], ps_x[:, :], kv_sum[:, :], ALU.add).then_inc(kv_added, 1)

            def blocks(a, batch, _):
                dve.wait_ge(kv_added, PER_BATCH * (batch + 1))
                V.tensor_tensor(kv_blocks[:, :, :], kv_sum[:, :].rearrange("p (c n) -> p c n", c=NC),
                                mask[:, None, :].to_broadcast([P, NC, P]), ALU.mult).then_inc(blocks_step, 1)
                dve.wait_ge(keys_step, N_KEYS * PER_BATCH * (batch + 1))
                for c in range(NC):
                    V.tensor_scalar(z_heads[:, c, :], head_of[:, c, :], z_sum[:, c:c + 1], None, ALU.mult
                                    ).then_inc(blocks_step, 1)

            def high1(j, batch, p):
                pair_taps(h1, xb, p, G0, j, h1_first, high1_step, (2 * j + p) * N_HIGH1)

            def dens(j, batch, _):
                dve.wait_ge(den_ready, j + 1)
                V.tensor_scalar(den[:, :], ps_y[0:HEADS, 0:QW], ATTN_EPS, None, ALU.add).then_inc(den_step, 1)
                dve.wait_ge(den_step, 2 * j + 1)
                V.reciprocal(den[:, :], den[:, :]).then_inc(den_step, 1)

            def attend(j, batch, c):
                dve.wait_ge(rden_out, NC * j + c + 1)
                V.tensor_tensor(att[:, c % 2, :], ps_x[:, 0:QW], att[:, c % 2, :], ALU.mult).then_inc(att_done, 1)

            def synth2(j, batch, c):
                n = (NC * j + c) * N_SYN2
                u = M2 + 1
                a_, h_ = att[:, c % 2, :], h2_in[:, c, :]
                odd, even = low[:, c % 2, 0:2 * u - 1:2], low[:, c % 2, 1:2 * u:2]
                dve.wait_ge(low_first, 2 * (NC * j + c + 1))
                tap(even, h_[:, 1:1 + u], c, T12).then_inc(syn2_step, 1)
                tap(odd, h_[:, 1:1 + u], c, T23).then_inc(syn2_step, 1)
                dve.wait_ge(syn2_step, n + 1)
                tap(even, h_[:, 2:2 + u], c, T0 + 3).then_inc(syn2_step, 1)
                dve.wait_ge(att_done, NC * j + c + 1)
                dve.wait_ge(syn2_step, n + 2)
                tap(odd, a_[:, 0:u], c, S01).then_inc(syn2_step, 1)
                dve.wait_ge(syn2_step, n + 3)
                tap(even, a_[:, 0:u], c, S0).then_inc(syn2_step, 1)
                dve.wait_ge(syn2_step, n + 4)
                tap(odd, a_[:, 1:1 + u], c, S23).then_inc(syn2_step, 1)
                dve.wait_ge(syn2_step, n + 5)
                tap(even, a_[:, 1:1 + u], c, S12).then_inc(syn2_step, 1)
                dve.wait_ge(syn2_step, n + 7)
                tap(even, a_[:, 2:2 + u], c, S0 + 3).then_inc(syn2_step, 1)
                dve.wait_ge(syn2_step, n + 8)
                edges(low[:, c % 2, :], j).then_inc(syn2_step, 1)

            def synth1a(j, batch, c):
                n = (NC * j + c) * N_SYN1
                even, odd = s_chan[:, c, 0:TOK - 1:2], s_chan[:, c, 1:TOK:2]
                dve.wait_ge(high1_step, (2 * j + c // 2 + 1) * N_HIGH1)
                if c == 0 and not first(j):
                    dve.wait_ge(s_ready, SUBS * j)
                tap(even, h1[:, c, 0:M1], c, T0, xb[:, c, 3:3 + TOK - 1:2]).then_inc(syn1_step, 1)
                tap(odd, h1[:, c, 1:1 + M1], c, T01, xb[:, c, 4:4 + TOK - 1:2]).then_inc(syn1_step, 1)
                dve.wait_ge(syn1_step, n + 1)
                tap(even, h1[:, c, 1:1 + M1], c, T12).then_inc(syn1_step, 1)
                dve.wait_ge(syn1_step, n + 2)
                tap(odd, h1[:, c, 2:2 + M1], c, T23).then_inc(syn1_step, 1)
                dve.wait_ge(syn1_step, n + 3)
                tap(even, h1[:, c, 2:2 + M1], c, T0 + 3).then_inc(syn1_step, 1)

            def synth1b(j, batch, c):
                n = (NC * j + c) * N_SYN1
                even, odd = s_chan[:, c, 0:TOK - 1:2], s_chan[:, c, 1:TOK:2]
                lw = low[:, c % 2, :]
                dve.wait_ge(syn2_step, (NC * j + c + 1) * N_SYN2)
                dve.wait_ge(syn1_step, n + 4)
                tap(odd, lw[:, 1:1 + M1], c, S01).then_inc(syn1_step, 1)
                dve.wait_ge(syn1_step, n + 5)
                tap(even, lw[:, 0:M1], c, S0).then_inc(syn1_step, 1)
                dve.wait_ge(syn1_step, n + 6)
                tap(odd, lw[:, 2:2 + M1], c, S23).then_inc(syn1_step, 1)
                dve.wait_ge(syn1_step, n + 7)
                tap(even, lw[:, 1:1 + M1], c, S12).then_inc(syn1_step, 1)
                dve.wait_ge(syn1_step, n + 9)
                tap(even, lw[:, 2:2 + M1], c, S0 + 3).then_inc(syn1_step, 1)

            def aggregate(dst, src, stats, value):
                hold(dve, stats, value)
                return V.bn_aggr(dst, src)

            def norm1(j, batch, t):
                s = SUBS * j + t
                dve.wait_ge(s_ready, s + 1)
                V.bn_stats(st1[:, t, :], ps_x[:, :]).then_inc(s_stats, 1)
                aggregate(mv1[:, t, :], st1[:, t, :], s_stats, s + 1).then_inc(s_mv, 1)
                dve.wait_ge(s_mv, s + 1)
                V.scalar_tensor_tensor(out=x1[:, t, :], in0=ps_x[:, :], scalar=mv1[:, t, 0:1],
                                       in1=gamma_b[:, :], op0=ALU.subtract, op1=ALU.mult).then_inc(s_centred, 1)

            def norm2(j, batch, t):
                s = SUBS * j + t
                dve.wait_ge(s_centred, s + 1)
                dve.wait_ge(x_beta, s + 1)
                dve.wait_ge(rstd1, s + 1)
                V.scalar_tensor_tensor(out=x1[:, t, :], in0=x1[:, t, :], scalar=rs1[:, t, 1:2],
                                       in1=xt[:, t % 4, :], op0=ALU.mult, op1=ALU.add,
                                       accum_out=rs2[:, t, 0:1]).then_inc(r_ready, 1)

            def norm3(j, batch, t):
                dve.wait_ge(x1_hi_ready, SUBS * j + t + 1)
                cols = slice((t % DSUB) * P, (t % DSUB + 1) * P)
                V.tensor_tensor(x1_lo[:, t // DSUB, :, cols], ps_y[:, :].rearrange("p (c n) -> p c n", c=NC),
                                x1_hi[:, t // DSUB, :, cols], ALU.subtract).then_inc(x1_lo_ready, 1)

            steps = {"low1": low1, "band2": band2, "keys": keys_sum, "kv": kv, "blocks": blocks, "high1": high1,
                     "dens": dens, "attend": attend, "synth2": synth2, "synth1a": synth1a, "synth1b": synth1b,
                     "norm1": norm1, "norm2": norm2, "norm3": norm3}

            def out1(a, batch, c):
                dve.wait_ge(l1_first, NC * a + c + 1)
                edges(l1[:, c, :], a).then_inc(low1_step, N_LOW1 // 2)

            def out2(a, batch, c):
                dve.wait_ge(band2_first, 2 * (NC * a + c + 1))
                V.tensor_scalar(keys[:, c, :], l2[:, c, :], 0.0, None, ALU.min).then_inc(band2_step, N_BAND2)

            def kv_add(a, batch, _):
                kv(a, batch, 0)
                if isinstance(a, int) and a == PER_BATCH - 1:
                    blocks(a, batch, 0)
                    dve.wait_ge(blocks_step, N_BLOCKS)
                    V.memset(kv_sum[:], 0.0).then_inc(sums_zero, 1)
                    V.memset(z_sum[:], 0.0).then_inc(sums_zero, 1)
                    dve.wait_ge(sums_zero, 2)

            before_analyses(dve, {**{name: steps[name] for name in steps if name != "kv"}, "out1": out1,
                                  "out2": out2, "kv_add": kv_add})
            run = before(steps)
            run(FIRST_MIX + FIRST_NORM, 0, 0)

            def body(i, batch, analysis, last):
                for b in range(2):
                    B = 2 * i + b
                    for k in range(NH):
                        n = NH * B + k
                        dve.wait_ge(silu_done, n + 1)
                        V.scalar_tensor_tensor(out=h_f[:, k % 2, :], in0=ps_gu[k % 2][1][:, :],
                                               scalar=WSCALE * H_SCALE / X1_SCALE, in1=gate_s[:, k % 2, :],
                                               op0=ALU.mult, op1=ALU.mult).then_inc(h_mul, 1)
                        beside(b, k, i, batch, analysis, last, steps)
                        dve.wait_ge(hi_done, n + 1)
                        V.tensor_tensor(h_lo[:, k, :], h_f[:, k % 2, :], h_hi[:, k, :], ALU.subtract
                                        ).then_inc(lo_done, 1)
                    for t in range(DSUB):
                        n = DSUB * B + t
                        beside(b, NH + t, i, batch, analysis, last, steps)
                        dve.wait_ge(d_ready, n + 1)
                        dve.wait_ge(st_out[t], 16 * (B + 1))
                        V.scalar_tensor_tensor(out=z[:, t, :], in0=ps_d[t % 2][:, :],
                                               scalar=WSCALE * X1_SCALE / H_SCALE, in1=x1[:, b * DSUB + t, :],
                                               op0=ALU.mult, op1=ALU.add, accum_out=rs3[:, t, 0:1]
                                               ).then_inc(z_done, 1)

            iterations(dve, body)


def kernel(L0_attn_x, L0_attn_h_filter, L0_attn_g_filter, L0_attn_h_synth, L0_attn_g_synth,
           L0_attn_norm_gamma, L0_attn_norm_beta, L0_ffn_w_gate, L0_ffn_w_up, L0_ffn_w_down):
    import numpy as np
    import concourse.bacc as bacc
    from concourse.bass_utils import run_bass_kernel_spmd

    x = np.ascontiguousarray(L0_attn_x)
    padded = np.zeros((P, BATCHES, NC, SEQ + 6), x.dtype)
    padded[:, :, :, 3:3 + SEQ] = x.reshape(BATCHES, SEQ, NC, P).transpose(3, 0, 2, 1)
    x_chan = np.stack([padded[:, j // PER_BATCH, :, j % PER_BATCH * TOK:j % PER_BATCH * TOK + XW]
                       for j in range(ITERS)], axis=1)
    taps = np.stack([np.asarray(f).reshape(4, NC, P) for f in
                     (L0_attn_h_filter, L0_attn_g_filter, L0_attn_h_synth, L0_attn_g_synth)])
    taps = np.ascontiguousarray(taps.transpose(3, 2, 0, 1).reshape(P, NC, 16))
    gamma = np.ascontiguousarray(np.broadcast_to(np.asarray(L0_attn_norm_gamma), (P, C)))
    beta = np.ascontiguousarray(np.broadcast_to(np.asarray(L0_attn_norm_beta), (P, C)))
    wg = np.asarray(L0_ffn_w_gate).reshape(HID, NC, P).transpose(2, 1, 0).reshape(P, NC * HID)
    wu = np.asarray(L0_ffn_w_up).reshape(HID, NC, P).transpose(2, 1, 0).reshape(P, NC * HID)
    wd = np.asarray(L0_ffn_w_down).reshape(C, NH, P).transpose(2, 1, 0).reshape(P, NH * C)
    weights = np.ascontiguousarray(np.concatenate([wg, wu, wd], axis=1))
    edge = np.ones((P, ITERS, 2), np.float32)
    edge[:, 0::PER_BATCH, 0] = 0.0
    edge[:, PER_BATCH - 1::PER_BATCH, 1] = 0.0
    edge = edge.reshape(P, 2 * ITERS)
    identity = np.eye(P, dtype=np.float32)
    block_mask = np.kron(np.eye(P // HEAD, dtype=np.float32), np.ones((HEAD, HEAD), np.float32))
    head_of = (np.arange(C) // HEAD)[:, None] == np.arange(HEADS)[None, :]
    head_mask = np.ascontiguousarray(head_of.reshape(NC, P, HEADS).transpose(1, 0, 2).astype(np.float32))
    head_spread = np.ascontiguousarray(head_of.reshape(NC, P, HEADS).transpose(2, 0, 1).astype(np.float32))

    nc = bacc.Bacc("TRN2", target_bir_lowering=False, num_devices=1, dynamic_dma_scratch_size=1024)
    arrays, args = {}, []
    for name, a in (("x_tok", x.reshape(BATCHES * SEQ, C)), ("x_chan", x_chan), ("taps", taps), ("gamma", gamma), ("beta", beta),
                    ("edge", edge), ("weights", weights), ("identity", identity), ("block_mask", block_mask),
                    ("head_mask", head_mask), ("head_spread", head_spread)):
        arrays[name] = a
        args.append(nc.dram_tensor(name, a.shape, mybir.dt.from_np(a.dtype), kind="ExternalInput").ap())
    out = nc.dram_tensor("out", (BATCHES * SEQ, C), F32, kind="ExternalOutput").ap()
    mixer_ffn(nc, *args, out)
    result = run_bass_kernel_spmd(nc, [arrays], core_ids=[0])
    return result.results[0]["out"].reshape(BATCHES, SEQ, C)
```

```python
from contextlib import ExitStack

import concourse.bass as bass
from concourse import mybir

P = 128
BATCHES, SEQ, C = 2, 4096, 512
HID = 1536
NC = C // P
NH = HID // P
TOK = 1024
PER_BATCH = SEQ // TOK
ITERS = BATCHES * PER_BATCH
BLK = 512
SUBS = TOK // P
DSUB = BLK // P
M1 = TOK // 2
M2 = TOK // 4
XW = TOK + 6
LW = M1 + 2
QW = M2 + 3
HEAD = 32
LN_EPS = 1e-5
ATTN_EPS = 1e-6
X1_SCALE = 2048.0
H_SCALE = 0.125
WSCALE = 1.0 / 127.0
PIECES = 12
PW = HID

F32 = mybir.dt.float32
F16 = mybir.dt.float16
I32 = mybir.dt.int32
ALU = mybir.AluOpType
ACT = mybir.ActivationFunctionType

H0, G0, S0, T0 = 0, 4, 8, 12
S12, S01, S23, T12, T01, T23 = 16, 17, 18, 19, 20, 21
NCOEF = 22

NEXT, NOW, ANA, LATE = "next iteration", "this iteration", "analysis", "close of the former analysis"
BESIDE = {
    (0, 0): [(NOW, "xbeta", 4), (NOW, "norm1", 4), (NOW, "norm1q", 4), (LATE, "keys", 0), (NEXT, "bands", 0),
             (NOW, "xbeta", 5)],
    (0, 1): [(NOW, "norm1", 5), (NOW, "norm1q", 5), (NOW, "norm2", 4), (NOW, "normq", 4),
             (ANA, "low1", 0)],
    (0, 2): [(NOW, "normx", 4), (NOW, "norm2", 5), (NOW, "normq", 5), (LATE, "turn", 0), (LATE, "turn", 1),
             (ANA, "low1", 1)],
    (0, 3): [(NOW, "normx", 5), (LATE, "turn", 2), (LATE, "turn", 3), (NOW, "xbeta", 6)],
    (0, 4): [(LATE, "kv", 0), (LATE, "blocks", 0), (NOW, "norm3", 4), (NOW, "xbeta", 7), (NEXT, "high1", 0)],
    (0, 5): [(NOW, "norm3", 5), (NOW, "norm1", 6), (NOW, "norm1q", 6)],
    (0, 6): [(NOW, "norm1", 7), (NOW, "norm1q", 7), (NOW, "norm2", 6), (NOW, "normq", 6), (NEXT, "high1", 1)],
    (0, 7): [(NOW, "normx", 6), (NOW, "norm2", 7), (NOW, "normq", 7)],
    (0, 8): [(NOW, "normx", 7), (NEXT, "dens", 0)],
    (0, 10): [(NOW, "norm3", 6), (NEXT, "synth1a", 0)],
    (0, 11): [(NOW, "norm3", 7), (NEXT, "synth1a", 1)],
    (0, 12): [(NEXT, "synth1a", 2)],
    (0, 13): [(NEXT, "attend", 0), (NEXT, "synth2", 0)],
    (0, 14): [(NEXT, "synth1a", 3)],
    (0, 15): [(NEXT, "attend", 1), (NEXT, "synth2", 1)],
    (1, 0): [(NEXT, "synth1b", 0)],
    (1, 1): [(NEXT, "attend", 2), (NEXT, "synth2", 2)],
    (1, 2): [(NEXT, "synth1b", 1)],
    (1, 3): [(NEXT, "attend", 3), (NEXT, "synth2", 3)],
    (1, 5): [(NEXT, "synth1b", 2), (NEXT, "xbeta", 0)],
    (1, 6): [(NEXT, "xbeta", 1)],
    (1, 7): [(NEXT, "synth1b", 3), (NEXT, "xbeta", 2)],
    (1, 8): [(ANA, "band2", 0), (NEXT, "xbeta", 3)],
    (1, 9): [(NEXT, "norm1", 0), (NEXT, "norm1q", 0), (ANA, "band2", 1)],
    (1, 10): [(NEXT, "norm1", 1), (NEXT, "norm1q", 1), (NEXT, "norm2", 0), (NEXT, "normq", 0), (ANA, "band2", 2)],
    (1, 11): [(NEXT, "norm1", 2), (NEXT, "norm1q", 2), (NEXT, "normx", 0), (NEXT, "norm2", 1), (NEXT, "normq", 1)],
    (1, 12): [(NEXT, "normx", 1), (NEXT, "norm2", 2), (NEXT, "normq", 2), (ANA, "band2", 3)],
    (1, 12.5): [(NEXT, "norm1", 3), (NEXT, "norm1q", 3)],
    (1, 13): [(NEXT, "norm3", 0), (NEXT, "normx", 2), (NEXT, "norm2", 3), (NEXT, "normq", 3)],
    (1, 14): [(NEXT, "norm3", 1), (NEXT, "normx", 3)],
    (1, 15): [(NEXT, "norm3", 2)],
    (1, 15.5): [(NEXT, "norm3", 3), (ANA, "exp", 0)],
}
THEN, THIS = "former analysis", "this analysis"
OPEN = [(THIS, "weights", 0), (THEN, "keys", 0), (THIS, "low1", 0), (THIS, "conv1", 2), (THIS, "out1", 2),
        (THEN, "turn", 0), (THEN, "turn", 1), (THIS, "conv1", 3), (THIS, "out1", 3), (THEN, "turn", 2),
        (THEN, "turn", 3), (THIS, "band2", 0), (THIS, "band2", 1), (THIS, "conv2", 2), (THIS, "cast", 0),
        (THEN, "kv", 0), (THIS, "conv2", 3), (THEN, "kv_add", 0), (THIS, "mix", 0), (THIS, "out2", 2), (THIS, "out2", 3),
        (THIS, "exp", 0)]
FIRST_MIX = [("dens", 0), ("h_conv", 2), ("attend", 0), ("h_conv", 3)]
for _c in range(NC):
    FIRST_MIX += [("synth2", _c)] + ([("attend", _c + 1)] if _c + 1 < NC else []) + \
                 [("synth1a", _c), ("synth1b", _c)] + ([("h_out", _c + 2)] if _c < 2 else [])
FIRST_NORM = [("xbeta", t) for t in range(DSUB)] + [(name, t) for t in range(DSUB) for name in ("norm1", "norm1q")]
for _s in range(DSUB + 3):
    FIRST_NORM += [(name, _s - lag) for name, lag in (("norm2", 0), ("normq", 0), ("normx", 1), ("norm3", 3))
                   if 0 <= _s - lag < DSUB]

N_HIGH1, N_LOW1, N_BAND2, N_SYN2, N_SYN1A, N_SYN1B, N_KEYS, N_BLOCKS = 8, 8, 7, 9, 5, 5, 5, 5
AHEAD = PER_BATCH + 1
HEADS = C // HEAD


def mixer_ffn(nc, x_tok, x_chan, taps, gamma, beta, edge, weights, identity, block_mask, head_mask, head_spread,
              out):
    q_dram = nc.dram_tensor("q_scratch", [P, BATCHES, NC, SEQ // 4 + 3], F32, kind="Internal").ap()
    h2_dram = nc.dram_tensor("h2_scratch", [P, BATCHES, NC, SEQ // 4 + 3], F32, kind="Internal").ap()

    with ExitStack() as ctx:
        def sb(name, shape, dt=F32):
            return ctx.enter_context(nc.sbuf_tensor(name, shape, dt))

        def sem(name):
            return ctx.enter_context(nc.semaphore(name))

        w16 = sb("w16", [P, PIECES * PW], F16)
        coef = sb("coef", [P, NC, NCOEF])
        gamma_b = sb("gamma_b", [P, C])
        beta_b = sb("beta_b", [P, C])
        edge_sb = sb("edge_sb", [P, 2 * ITERS])
        ident = sb("ident", [P, P])
        mask = sb("mask", [P, P])
        zeros = sb("zeros", [P, 16])
        minus_half = sb("minus_half", [P, 1])
        xa = sb("xa", [P, NC, XW])
        l1 = sb("l1", [P, NC, LW])
        l2 = sb("l2", [P, NC, M2])
        h2 = sb("h2", [P, NC, M2])
        keys = sb("keys", [P, NC, M2])
        kv_sum = sb("kv_sum", [P, NC * P])
        z_part = sb("z_part", [P, NC])
        z_sum = sb("z_sum", [P, NC])
        kv_blocks = sb("kv_blocks", [P, NC, P])
        z_heads = sb("z_heads", [P, NC, HEADS])
        head_of = sb("head_of", [P, NC, HEADS])
        spread = sb("spread", [HEADS, NC, P])
        den = sb("den", [HEADS, QW])
        xb = sb("xb", [P, NC, XW])
        q_in = sb("q_in", [P, NC, QW])
        h2_in = sb("h2_in", [P, NC, QW])
        h1_mem = sb("h1_mem", [P, NC * LW])
        h1 = h1_mem[:, :].rearrange("p (c n) -> p c n", c=NC)
        kvt = h1_mem[:, 0:NC * 4 * P].rearrange("p (c n) -> p c n", c=NC)
        low = sb("low", [P, 2, LW])
        att = sb("att", [P, 2, QW])
        xt = sb("xt", [P, 4, C])
        s_chan = sb("s_chan", [P, NC, TOK])
        x1 = sb("x1", [P, SUBS, C])
        junk = sb("junk", [P, C], F16)
        rs1 = sb("rs1", [P, SUBS, 5])
        rs2 = sb("rs2", [P, SUBS, 6])
        x1_hi = sb("x1_hi", [P, 2, NC, BLK], F16)
        x1_lo = sb("x1_lo", [P, 2, NC, BLK], F16)
        hid = sb("hid", [P, 2 * NH * BLK], F16)
        h_hi = hid[:, 0:NH * BLK].rearrange("p (k n) -> p k n", k=NH)
        h_lo = hid[:, NH * BLK:2 * NH * BLK].rearrange("p (k n) -> p k n", k=NH)
        stage = hid[:, :].bitcast(I32)
        gate_s = sb("gate_s", [P, 2, BLK])
        h_f = sb("h_f", [P, 2, BLK])
        z = sb("z", [P, DSUB, C])
        rs3 = sb("rs3", [P, DSUB, 6])
        minus_part = sb("minus_part", [P, 1])

        ps_gu = [[ctx.enter_context(nc.psum_tensor(f"ps_{n}{k}", [P, BLK], F32)) for n in ("gate", "up")]
                 for k in range(2)]
        ps_d = [ctx.enter_context(nc.psum_tensor(f"ps_down{k}", [P, C], F32)) for k in range(2)]
        ps_x = ctx.enter_context(nc.psum_tensor("ps_x", [P, 512], F32))
        ps_y = ctx.enter_context(nc.psum_tensor("ps_y", [P, 512], F32))

        ld_const, zero_pads = sem("ld_const"), sem("zero_pads")
        ld_w = [sem(f"ld_w{n}") for n in range(3)]
        ld_xa = [sem(f"ld_xa{c}") for c in range(NC)]
        ld_xb, ld_q, ld_h2 = sem("ld_xb"), sem("ld_q"), sem("ld_h2")
        ld_xt = [sem(f"ld_xt{n}") for n in range(4)]
        st_q, st_h2 = sem("st_q"), sem("st_h2")
        st_out = [sem(f"st_out{t}") for t in range(DSUB)]
        set_dve, set_pool, coef_ready, w_cast = sem("set_dve"), sem("set_pool"), sem("coef_ready"), sem("w_cast")
        sums_zero = sem("sums_zero")
        l1_first, band2_first, low1_step, band2_step = (sem("l1_first"), sem("band2_first"), sem("low1_step"),
                                                        sem("band2_step"))
        exp_done, keys_step, turned, turn_out = sem("exp_done"), sem("keys_step"), sem("turned"), sem("turn_out")
        kv_ready, kv_added, blocks_step = sem("kv_ready"), sem("kv_added"), sem("blocks_step")
        diag_ready, conv1_ready, conv2_ready = sem("diag_ready"), sem("conv1_ready"), sem("conv2_ready")
        h_conv_ready = sem("h_conv_ready")
        h1_first, low_first, high1_step = sem("h1_first"), sem("low_first"), sem("high1_step")
        den_ready, den_step, qk_ready, rden_out, att_done = (sem("den_ready"), sem("den_step"), sem("qk_ready"),
                                                             sem("rden_out"), sem("att_done"))
        syn2_step, syn1a_step, syn1b_step = sem("syn2_step"), sem("syn1a_step"), sem("syn1b_step")
        s_ready, s_out, nmean1, s_squares, s_centred = (sem("s_ready"), sem("s_out"), sem("nmean1"),
                                                        sem("s_squares"), sem("s_centred"))
        var1, rstd1, x_beta = sem("var1"), sem("rstd1"), sem("x_beta")
        r_ready, nmean2, r_squares, var2, rstd2, shift2 = (sem("r_ready"), sem("nmean2"), sem("r_squares"),
                                                           sem("var2"), sem("rstd2"), sem("shift2"))
        x1_ready, x1_turned, x1_hi_ready, x1_lo_ready = (sem("x1_ready"), sem("x1_turned"), sem("x1_hi_ready"),
                                                         sem("x1_lo_ready"))
        gu_ready, silu_done, h_mul, hi_done, lo_done = (sem("gu_ready"), sem("silu_done"), sem("h_mul"),
                                                        sem("hi_done"), sem("lo_done"))
        d_ready, z_done, nmean3, z_squares = sem("d_ready"), sem("z_done"), sem("nmean3"), sem("z_squares")
        var3, rstd3, shift3, out_done = sem("var3"), sem("rstd3"), sem("shift3"), sem("out_done")

        def hold(eng, semaphore, value):
            eng.wait_ge(semaphore, value)
            eng.nop(nofuse=True)

        def before(steps):
            def run(names, index, batch):
                for name, n in names:
                    if name in steps:
                        steps[name](index, batch, n)
            return run

        def diag(n):
            return z[:, n // 4, (n % 4) * P:(n % 4 + 1) * P]

        def before_analyses(eng, steps):
            def analysis(a, batch=0):
                for which, name, n in OPEN:
                    if name not in steps:
                        continue
                    if which is THIS:
                        steps[name](a, batch, n)
                    elif not first(a):
                        steps[name](a - 1, 0, n)

            analysis(0)
            analysis(1)
            with eng.Fori(2, PER_BATCH) as a:
                analysis(a)
            analysis(PER_BATCH, 1)

        def first(index):
            return isinstance(index, int) and index == 0

        def closed_before(j, batch):
            return batch == 0 or (isinstance(j, int) and j == PER_BATCH)

        def iterations(eng, body):
            with eng.Fori(0, 2) as i:
                body(i, 0, True, False)
            body(2, 0, True, True)
            body(3, 0, False, True)
            with eng.Fori(PER_BATCH, ITERS - 1) as i:
                body(i, 1, False, False)
            body(ITERS - 1, 1, False, True)

        def beside(b, k, i, batch, analysis, last, steps):
            for which, name, n in BESIDE.get((b, k), []):
                if name not in steps:
                    continue
                if which is NOW:
                    steps[name](i, batch, n)
                elif which is NEXT and not (last and batch == 1):
                    steps[name](i + 1, batch + (1 if last and not analysis else 0), n)
                elif which is ANA and analysis:
                    steps[name](i + AHEAD, 1, n)
                elif which is LATE and batch == 0 and (name != "blocks" or not analysis):
                    steps[name](i + PER_BATCH, 1, n)

        block = ctx.enter_context(nc.Block())

        @block.sync
        def _(sp):
            def load_xa(a, c):
                sp.dma_start(xa[:, c, :], x_chan[:, bass.ds(a, 1), c, :]).then_inc(ld_xa[c], 16)

            def low1(a, batch, p):
                if isinstance(a, int) and a == ITERS - 1:
                    return
                hold(sp, low1_step, (2 * a + p) * N_LOW1 + 6)
                load_xa(a + 1, 2 * p)
                load_xa(a + 1, 2 * p + 1)

            def keys_store(a, batch, _):
                at = (a - PER_BATCH * batch) * M2 + 1
                hold(sp, band2_step, (a + 1) * NC * N_BAND2)
                sp.dma_start(h2_dram[:, batch, :, bass.ds(at, M2)], h2[:, :, :]).then_inc(st_h2, 16)
                hold(sp, keys_step, (a + 1) * N_KEYS)
                sp.dma_start(q_dram[:, batch, :, bass.ds(at, M2)], keys[:, :, :]).then_inc(st_q, 16)

            def load_xb(j):
                sp.dma_start(xb[:, :, :], x_chan[:, bass.ds(j, 1), :, :].rearrange("p a c n -> p (a c) n")
                             ).then_inc(ld_xb, 16)

            def load_bands(j, batch):
                at = (j - PER_BATCH * batch) * M2
                hold(sp, st_q, 16 * PER_BATCH * (batch + 1))
                hold(sp, st_h2, 16 * PER_BATCH * (batch + 1))
                sp.dma_start(q_in[:, :, :], q_dram[:, batch, :, bass.ds(at, QW)]).then_inc(ld_q, 16)
                sp.dma_start(h2_in[:, :, :], h2_dram[:, batch, :, bass.ds(at, QW)]).then_inc(ld_h2, 16)

            def load_xt(j, t):
                sp.dma_start(xt[:, t % 4, :], x_tok[bass.ds(j * TOK + t * P, P), :]).then_inc(ld_xt[t % 4], 16)

            def after_norm2(j, batch, t):
                if isinstance(j, int) and j == ITERS - 1 and t >= 4:
                    return
                hold(sp, r_ready, SUBS * j + t + 1)
                load_xt(j + (t + 4) // SUBS, (t + 4) % SUBS)

            def load_weights(a, batch, _):
                if isinstance(a, int) and a == PER_BATCH:
                    return
                for n in range(3):
                    if not first(a):
                        hold(sp, w_cast, 3 * a)
                    sp.dma_start(stage[:, n * PW:(n + 1) * PW], weights[:, bass.ds((a * 3 + n) * PW, PW)]
                                 ).then_inc(ld_w[n], 16)

            def out1(a, batch, c):
                if c == 3:
                    low1(a, batch, 1)

            def first_bands(a, batch, _):
                if isinstance(a, int) and a == PER_BATCH - 1:
                    hold(sp, zero_pads, 64)
                    load_bands(0, 0)
                    for t in range(4):
                        load_xt(0, t)

            def next_bands(j, batch, _):
                hold(sp, syn2_step, N_SYN2 * NC * j)
                load_bands(j, batch)

            steps = {"low1": low1, "keys": keys_store, "norm2": after_norm2, "bands": next_bands}
            run = before(steps)

            for c in range(NC):
                load_xa(0, c)
            for dst, src in ((coef[:, :, 0:16], taps), (edge_sb[:, :], edge), (ident[:, :], identity),
                             (mask[:, :], block_mask), (head_of[:, :, :], head_mask),
                             (spread[:, :, :], head_spread), (gamma_b[:, :], gamma), (beta_b[:, :], beta)):
                sp.dma_start(dst, src).then_inc(ld_const, 16)
            hold(sp, set_dve, 1)
            for dram in (q_dram, h2_dram):
                for at, width in ((0, 1), (SEQ // 4 + 1, 2)):
                    sp.dma_start(dram[:, :, :, at:at + width], zeros[:, 0:8 * width].rearrange(
                        "p (b c w) -> p b c w", b=BATCHES, c=NC), allow_slow_non_contiguous=True
                        ).then_inc(zero_pads, 16)
            load_xb(0)
            before_analyses(sp, {**steps, "out1": out1, "weights": load_weights, "kv": first_bands})
            run(FIRST_NORM, 0, 0)

            def body(i, batch, analysis, last):
                more = not (last and batch == 1)
                for b in range(2):
                    for k in range(NH + DSUB):
                        if (b, k) == (0, 0) and more:
                            hold(sp, syn1a_step, N_SYN1A * NC * (i + 1))
                            load_xb(i + 1)
                        beside(b, k, i, batch, analysis, last, steps)
                        if k >= NH:
                            t = k - NH
                            B = 2 * i + b
                            hold(sp, out_done, DSUB * B + t + 1)
                            sp.dma_start(out[bass.ds(B * BLK + t * P, P), :], z[:, t, :]).then_inc(st_out[t], 16)

            iterations(sp, body)
            for t in range(DSUB):
                hold(sp, st_out[t], 16 * (2 * ITERS + 1))

        @block.tensor
        def _(pe):
            def turn(a, batch, c):
                bank = (ps_x, ps_y)[c % 2]
                if c == 0:
                    pe.wait_ge(keys_step, (a + 1) * N_KEYS - 1)
                    if batch == 1:
                        pe.wait_ge(s_out, SUBS * (a - PER_BATCH) + 6)
                    elif not first(a):
                        pe.wait_ge(kv_added, a)
                if c == 1 and batch == 1:
                    pe.wait_ge(x1_lo_ready, SUBS * (a - PER_BATCH) + 4)
                if c >= 2:
                    pe.wait_ge(turn_out, NC * a + c - 1)
                for n, src in enumerate((keys[:, c, 0:P], keys[:, c, P:2 * P], l2[:, c, 0:P], l2[:, c, P:2 * P])):
                    mm = pe.transpose(bank[:, n * P:(n + 1) * P], src, ident[:, :])
                mm.then_inc(turned, 1)

            def kv(a, batch, _):
                pe.wait_ge(turn_out, NC * (a + 1))
                for c in range(NC):
                    for n in range(2):
                        mm = pe.matmul(ps_x[:, c * P:(c + 1) * P], kvt[:, c, n * P:(n + 1) * P],
                                       kvt[:, c, (2 + n) * P:(3 + n) * P], start=(n == 0), stop=(n == 1))
                mm.then_inc(kv_ready, 1)

            def dens(j, batch, _):
                pe.wait_ge(ld_q, 16 * (j + 1))
                pe.wait_ge(blocks_step, N_BLOCKS * (batch + 1))
                if first(j):
                    pe.wait_ge(turn_out, NC * PER_BATCH)
                else:
                    pe.wait_ge(x1_lo_ready, SUBS * j - 2)
                for c in range(NC):
                    mm = pe.matmul(ps_y[0:HEADS, 0:QW], z_heads[:, c, :], q_in[:, c, :], start=(c == 0),
                                   stop=(c == NC - 1))
                mm.then_inc(den_ready, 1)

            def attend(j, batch, c):
                if c == 0:
                    pe.wait_ge(den_step, 2 * (j + 1))
                    if first(j):
                        pe.wait_ge(kv_added, PER_BATCH)
                    else:
                        pe.wait_ge(x1_lo_ready, SUBS * j)
                        pe.wait_ge(s_out, SUBS * j)
                else:
                    pe.wait_ge(att_done, NC * j + c)
                pe.matmul(ps_y[:, 0:QW], spread[:, c, :], den[:, :], start=True, stop=True)
                pe.matmul(ps_x[:, 0:QW], kv_blocks[:, c, :], q_in[:, c, :], start=True, stop=True
                          ).then_inc(qk_ready, 1)

            def norm1(j, batch, t):
                if t == 0:
                    pe.wait_ge(syn1b_step, N_SYN1B * NC * (j + 1))
                    pe.wait_ge(att_done, NC * (j + 1))
                else:
                    pe.wait_ge(s_out, SUBS * j + t)
                if t == 6 and batch == 0:
                    pe.wait_ge(kv_added, j + PER_BATCH + 1)
                for c in range(NC):
                    mm = pe.transpose(ps_x[:, c * P:(c + 1) * P], s_chan[:, c, t * P:(t + 1) * P], ident[:, :])
                mm.then_inc(s_ready, 1)

            def norm3(j, batch, t):
                s = SUBS * j + t
                pe.wait_ge(x1_ready, s + 1)
                if t == 0:
                    pe.wait_ge(att_done, NC * (j + 1))
                else:
                    pe.wait_ge(x1_lo_ready, s)
                if t == 6 and not (isinstance(j, int) and j == ITERS - 1):
                    pe.wait_ge(den_step, 2 * (j + 1) + 1)
                if t == 4 and batch == 0:
                    pe.wait_ge(turn_out, NC * (j + PER_BATCH + 1))
                for c in range(NC):
                    mm = pe.transpose(ps_y[:, c * P:(c + 1) * P], x1[:, t, c * P:(c + 1) * P], ident[:, :])
                mm.then_inc(x1_turned, 1)

            steps = {"turn": turn, "kv": kv, "dens": dens, "attend": attend, "norm1": norm1, "norm3": norm3}

            def gate_up(B, b, k):
                if k == 0:
                    pe.wait_ge(x1_hi_ready, DSUB * (B + 1))
                    pe.wait_ge(x1_lo_ready, DSUB * (B + 1))
                pe.wait_ge(h_mul, NH * B + k + 1)
                for g in range(2):
                    for c in range(NC):
                        w = w16[:, (g * NC + c) * PW + k * P:(g * NC + c) * PW + (k + 1) * P]
                        pe.matmul(ps_gu[k % 2][g][:, :], w, x1_hi[:, b, c, :], start=(c == 0), stop=False)
                        mm = pe.matmul(ps_gu[k % 2][g][:, :], w, x1_lo[:, b, c, :], start=False, stop=(c == NC - 1))
                mm.then_inc(gu_ready, 1)

            def down(B, t, chunks):
                if chunks[0] == 0:
                    pe.wait_ge(z_done, DSUB * B + t + 1)
                for k in chunks:
                    if t == 0 and k >= NH - 3:
                        pe.wait_ge(hi_done, NH * B + k + 1)
                        pe.wait_ge(lo_done, NH * B + k + 1)
                    elif t == 0 and k == 0:
                        pe.wait_ge(hi_done, NH * B + NH - 3)
                        pe.wait_ge(lo_done, NH * B + NH - 3)
                    w = w16[:, 2 * NC * PW + k * C:2 * NC * PW + (k + 1) * C]
                    pe.matmul(ps_d[t % 2][:, :], h_hi[:, k, t * P:(t + 1) * P], w, start=(k == 0), stop=False)
                    mm = pe.matmul(ps_d[t % 2][:, :], h_lo[:, k, t * P:(t + 1) * P], w, start=False,
                                   stop=(k == NH - 1))
                if chunks[-1] == NH - 1:
                    mm.then_inc(d_ready, 1)

            def body(i, batch, analysis, last):
                for b in range(2):
                    for k in range(NH):
                        gate_up(2 * i + b, b, k)
                        beside(b, k, i, batch, analysis, last, steps)
                    for t in range(DSUB):
                        beside(b, NH + t, i, batch, analysis, last, steps)
                        down(2 * i + b, t, range(NH // 2))
                        beside(b, NH + t + 0.5, i, batch, analysis, last, steps)
                        down(2 * i + b, t, range(NH // 2, NH))

            def conv1(a, batch, c):
                half = LW // 2
                pe.wait_ge(ld_xa[c], 16 * (a + 1))
                for n in range(2):
                    for k in range(4):
                        at = 2 * n * half + k
                        mm = pe.matmul(ps_gu[c - 2][n][:, 0:half], diag(8 * (c - 2) + k),
                                       xa[:, c, at:at + 2 * half - 1:2], start=(k == 0), stop=(k == 3))
                mm.then_inc(conv1_ready, 1)

            def conv2(a, batch, c):
                pe.wait_ge(low1_step, (2 * a + 2) * N_LOW1)
                for g in range(2):
                    for k in range(4):
                        mm = pe.matmul(ps_d[c - 2][:, g * M2:(g + 1) * M2], diag(8 * (c - 2) + 4 * g + k),
                                       l1[:, c, k:k + 2 * M2 - 1:2], start=(k == 0), stop=(k == 3))
                mm.then_inc(conv2_ready, 1)

            def h_conv(j, batch, c):
                half = LW // 2
                pe.wait_ge(ld_xb, 16)
                pe.wait_ge(l1_first, NC * PER_BATCH + c + 1)
                for n in range(2):
                    for k in range(4):
                        at = 2 * n * half + k
                        mm = pe.matmul(ps_gu[c - 2][n][:, 0:half], diag(8 * (c - 2) + 4 + k),
                                       xb[:, c, at:at + 2 * half - 1:2], start=(k == 0), stop=(k == 3))
                mm.then_inc(h_conv_ready, 1)

            pe.wait_ge(ld_const, 128)
            pe.wait_ge(diag_ready, 16)
            before_analyses(pe, {**steps, "conv1": conv1, "conv2": conv2})
            run = before({**steps, "h_conv": h_conv})
            run(FIRST_MIX + FIRST_NORM, 0, 0)
            pe.wait_ge(w_cast, PIECES)
            iterations(pe, body)

        @block.scalar
        def _(act):
            def first_tap(dst, src, c, tap, done):
                nc.scalar.activation(dst, src, ACT.Copy, scale=coef[:, c, tap:tap + 1]).then_inc(done, 1)

            def low1(a, batch, p):
                for c in (2 * p, 2 * p + 1):
                    act.wait_ge(ld_xa[c], 16 * (a + 1))
                    if c == 0 and not first(a):
                        act.wait_ge(band2_step, NC * N_BAND2 * a)
                    first_tap(l1[:, c, :], xa[:, c, 0:2 * LW - 1:2], c, H0, l1_first)

            def band2(a, batch, c):
                act.wait_ge(low1_step, (2 * a + c // 2 + 1) * N_LOW1)
                if c == 0 and not first(a):
                    act.wait_ge(keys_step, N_KEYS * a)
                    act.wait_ge(turned, NC * a)
                    act.wait_ge(st_h2, 16 * a)
                first_tap(l2[:, c, :], l1[:, c, 0:2 * M2 - 1:2], c, H0, band2_first)
                first_tap(h2[:, c, :], l1[:, c, 0:2 * M2 - 1:2], c, G0, band2_first)

            def exp(a, batch, _):
                act.wait_ge(band2_step, NC * N_BAND2 * (a + 1))
                nc.scalar.activation(keys[:, :, :], keys[:, :, :], ACT.Exp).then_inc(exp_done, 1)

            def turn(a, batch, c):
                act.wait_ge(turned, NC * a + c + 1)
                if c == 0:
                    if batch == 1:
                        act.wait_ge(syn1a_step, N_SYN1A * NC * (a - PER_BATCH + 1))
                    if not first(a):
                        act.wait_ge(kv_ready, a)
                nc.scalar.activation(kvt[:, c, :], (ps_x, ps_y)[c % 2][:, :], ACT.Copy).then_inc(turn_out, 1)

            def high1(j, batch, p):
                if p == 0:
                    act.wait_ge(ld_xb, 16 * (j + 1))
                    if not first(j):
                        act.wait_ge(syn1a_step, N_SYN1A * NC * j)
                    if closed_before(j, batch):
                        act.wait_ge(kv_ready, j + PER_BATCH)
                for c in (2 * p, 2 * p + 1):
                    first_tap(h1[:, c, :], xb[:, c, 0:2 * LW - 1:2], c, G0, h1_first)

            def synth2(j, batch, c):
                if c == 0:
                    act.wait_ge(ld_h2, 16 * (j + 1))
                if not (isinstance(j, int) and NC * j + c < 2):
                    act.wait_ge(syn1b_step, N_SYN1B * (NC * j + c - 1))
                u = M2 + 1
                first_tap(low[:, c % 2, 0:2 * u - 1:2], h2_in[:, c, 0:u], c, T01, low_first)
                first_tap(low[:, c % 2, 1:2 * u:2], h2_in[:, c, 0:u], c, T0, low_first)

            def attend(j, batch, c):
                act.wait_ge(qk_ready, NC * j + c + 1)
                if not (isinstance(j, int) and NC * j + c < 2):
                    act.wait_ge(syn2_step, N_SYN2 * (NC * j + c - 1))
                nc.scalar.activation(att[:, c % 2, :], ps_y[:, 0:QW], ACT.Copy).then_inc(rden_out, 1)

            def norm1(j, batch, t):
                act.wait_ge(s_ready, SUBS * j + t + 1)
                nc.scalar.activation(x1[:, t, :], ps_x[:, :], ACT.Copy, accum_out=rs1[:, t, 0:1]).then_inc(s_out, 1)

            def norm1q(j, batch, t):
                act.wait_ge(nmean1, SUBS * j + t + 1)
                nc.scalar.activation(junk[:, :], x1[:, t, :], ACT.Square, bias=rs1[:, t, 1:2],
                                     accum_out=rs1[:, t, 2:3]).then_inc(s_squares, 1)

            def normq(j, batch, t):
                act.wait_ge(nmean2, SUBS * j + t + 1)
                nc.scalar.activation(junk[:, :], x1[:, t, :], ACT.Square, bias=rs2[:, t, 1:2],
                                     accum_out=rs2[:, t, 2:3]).then_inc(r_squares, 1)

            def normx(j, batch, t):
                act.wait_ge(shift2, SUBS * j + t + 1)
                act.wait_ge(r_squares, SUBS * j + t + 1)
                nc.scalar.activation(x1[:, t, :], x1[:, t, :], ACT.Identity, bias=rs2[:, t, 5:6],
                                     scale=rs2[:, t, 4:5]).then_inc(x1_ready, 1)

            def norm3(j, batch, t):
                act.wait_ge(x1_turned, SUBS * j + t + 1)
                nc.scalar.activation(x1_hi[:, t // DSUB, :, (t % DSUB) * P:(t % DSUB + 1) * P],
                                     ps_y[:, :].rearrange("p (c n) -> p c n", c=NC), ACT.Copy
                                     ).then_inc(x1_hi_ready, 1)

            early = {"low1": low1, "band2": band2, "high1": high1, "attend": attend, "synth2": synth2,
                     "norm1": norm1, "norm3": norm3, "turn": turn}
            late = {"exp": exp, "norm1q": norm1q, "normq": normq, "normx": normx}

            def out1(a, batch, c):
                half = LW // 2
                act.wait_ge(conv1_ready, 2 * a + c - 1)
                nc.scalar.activation(l1[:, c, 0:half], ps_gu[c - 2][0][:, 0:half], ACT.Copy)
                nc.scalar.activation(l1[:, c, half:LW], ps_gu[c - 2][1][:, 0:half], ACT.Copy
                                     ).then_inc(l1_first, 1)

            def out2(a, batch, c):
                act.wait_ge(conv2_ready, 2 * a + c - 1)
                for g, band in enumerate((l2, h2)):
                    nc.scalar.activation(band[:, c, :], ps_d[c - 2][:, g * M2:(g + 1) * M2], ACT.Copy
                                         ).then_inc(band2_first, 1)

            def cast_weights(a, batch, _):
                if isinstance(a, int) and a == PER_BATCH:
                    return
                for n in range(3):
                    act.wait_ge(ld_w[n], 16 * (a + 1))
                    nc.scalar.activation(w16[:, bass.ds((a * 3 + n) * PW, PW)], stage[:, n * PW:(n + 1) * PW],
                                         ACT.Copy).then_inc(w_cast, 1)

            def first_high(a, batch, _):
                if isinstance(a, int) and a == PER_BATCH:
                    high1(0, 0, 0)

            def h_out(j, batch, c):
                half = LW // 2
                act.wait_ge(h_conv_ready, c - 1)
                nc.scalar.activation(h1[:, c, 0:half], ps_gu[c - 2][0][:, 0:half], ACT.Copy)
                nc.scalar.activation(h1[:, c, half:LW], ps_gu[c - 2][1][:, 0:half], ACT.Copy
                                     ).then_inc(h1_first, 1)

            act.wait_ge(coef_ready, 6)
            before_analyses(act, {**early, **late, "out1": out1, "out2": out2, "cast": cast_weights,
                                  "mix": first_high})
            run = before({**early, **late, "h_out": h_out})
            run(FIRST_MIX + FIRST_NORM, 0, 0)

            def square(B, t):
                act.wait_ge(nmean3, DSUB * B + t + 1)
                nc.scalar.activation(junk[:, :], z[:, t, :], ACT.Square, bias=rs3[:, t, 1:2],
                                     accum_out=rs3[:, t, 2:3]).then_inc(z_squares, 1)

            def normalise(B, t):
                act.wait_ge(shift3, DSUB * B + t + 1)
                nc.scalar.activation(z[:, t, :], z[:, t, :], ACT.Identity, bias=rs3[:, t, 5:6],
                                     scale=rs3[:, t, 4:5]).then_inc(out_done, 1)

            def body(i, batch, analysis, last):
                for b in range(2):
                    B = 2 * i + b
                    for k in range(NH):
                        act.wait_ge(gu_ready, NH * B + k + 1)
                        nc.scalar.activation(gate_s[:, k % 2, :], ps_gu[k % 2][0][:, :], ACT.Silu,
                                             scale=WSCALE / X1_SCALE).then_inc(silu_done, 1)
                        beside(b, k, i, batch, analysis, last, early)
                        act.wait_ge(h_mul, NH * B + k + 3)
                        nc.scalar.activation(h_hi[:, k, :], h_f[:, k % 2, :], ACT.Copy).then_inc(hi_done, 1)
                        beside(b, k, i, batch, analysis, last, late)
                    for t in range(DSUB):
                        beside(b, NH + t, i, batch, analysis, last, early)
                        if t > 0:
                            square(B, t - 1)
                        beside(b, NH + t, i, batch, analysis, last, late)
                        if t > 0:
                            normalise(B, t - 1)
                        beside(b, NH + t + 0.5, i, batch, analysis, last, early)
                        beside(b, NH + t + 0.5, i, batch, analysis, last, late)
                    square(B, DSUB - 1)
                    normalise(B, DSUB - 1)

            iterations(act, body)

        @block.gpsimd
        def _(pool):
            nc.gpsimd.memset(minus_half[:], -0.5).then_inc(set_pool, 1)
            nc.gpsimd.memset(minus_part[:], -1.0 / C).then_inc(set_pool, 1)
            pool.wait_ge(set_pool, 2)
            pool.wait_ge(ld_const, 128)
            for n in range(16):
                c = 2 + n // 8
                nc.gpsimd.tensor_tensor(diag(n), ident[:, :], coef[:, c, n % 8:n % 8 + 1].to_broadcast([P, P]), ALU.mult
                                        ).then_inc(diag_ready, 1)

            def xbeta(j, batch, t):
                pool.wait_ge(ld_xt[t % 4], 16 * (2 * j + t // 4 + 1))
                nc.gpsimd.tensor_tensor(xt[:, t % 4, :], xt[:, t % 4, :], beta_b[:, :], ALU.add
                                        ).then_inc(x_beta, 1)

            def norm1(j, batch, t):
                pool.wait_ge(s_out, SUBS * j + t + 1)
                nc.gpsimd.tensor_tensor(rs1[:, t, 1:2], rs1[:, t, 0:1], minus_part[:, :], ALU.mult
                                        ).then_inc(nmean1, 1)

            def norm1q(j, batch, t):
                n = SUBS * j + t + 1
                rs = rs1[:, t, :]
                hold(pool, s_squares, n)
                nc.gpsimd.tensor_scalar(rs[:, 3:4], rs[:, 2:3], 1.0 / C, LN_EPS, ALU.mult, ALU.add
                                        ).then_inc(var1, 1)
                pool.wait_ge(var1, n)
                nc.gpsimd.tensor_tensor(rs[:, 4:5], rs[:, 3:4], minus_half[:, :], ALU.pow).then_inc(rstd1, 1)

            def norm2(j, batch, t):
                pool.wait_ge(r_ready, SUBS * j + t + 1)
                nc.gpsimd.tensor_tensor(rs2[:, t, 1:2], rs2[:, t, 0:1], minus_part[:, :], ALU.mult
                                        ).then_inc(nmean2, 1)

            def scale_and_shift(rs, n, squares, eps, shrink, var, rstd, shift):
                hold(pool, squares, n)
                nc.gpsimd.tensor_scalar(rs[:, 3:4], rs[:, 2:3], shrink / C, eps * shrink, ALU.mult, ALU.add
                                        ).then_inc(var, 1)
                pool.wait_ge(var, n)
                nc.gpsimd.tensor_tensor(rs[:, 4:5], rs[:, 3:4], minus_half[:, :], ALU.pow).then_inc(rstd, 1)
                pool.wait_ge(rstd, n)
                nc.gpsimd.tensor_tensor(rs[:, 5:6], rs[:, 1:2], rs[:, 4:5], ALU.mult).then_inc(shift, 1)

            def normq(j, batch, t):
                scale_and_shift(rs2[:, t, :], SUBS * j + t + 1, r_squares, LN_EPS, X1_SCALE ** -2,
                                var2, rstd2, shift2)

            steps = {"norm1": norm1, "norm1q": norm1q, "xbeta": xbeta, "norm2": norm2, "normq": normq}
            before(steps)(FIRST_NORM, 0, 0)

            def body(i, batch, analysis, last):
                for b in range(2):
                    for k in range(NH + DSUB):
                        beside(b, k, i, batch, analysis, last, steps)
                        if k >= NH:
                            t = k - NH
                            n = DSUB * (2 * i + b) + t + 1
                            beside(b, k + 0.5, i, batch, analysis, last, steps)
                            pool.wait_ge(z_done, n + 2)
                            nc.gpsimd.tensor_tensor(rs3[:, t, 1:2], rs3[:, t, 0:1], minus_part[:, :], ALU.mult
                                                    ).then_inc(nmean3, 1)
                            scale_and_shift(rs3[:, t, :], n, z_squares, LN_EPS * X1_SCALE ** 2, 1.0,
                                            var3, rstd3, shift3)

            iterations(pool, body)

        @block.vector
        def _(dve):
            V = nc.vector
            V.memset(zeros[:], 0.0).then_inc(set_dve, 1)
            V.memset(kv_sum[:], 0.0).then_inc(h_mul, 2)
            V.memset(z_sum[:], 0.0).then_inc(z_done, 2)
            dve.wait_ge(ld_const, 128)
            for dst, a, b in ((S12, S0 + 1, S0 + 2), (S01, S0, S0 + 1), (S23, S0 + 2, S0 + 3),
                              (T12, T0 + 1, T0 + 2), (T01, T0, T0 + 1), (T23, T0 + 2, T0 + 3)):
                V.tensor_tensor(coef[:, :, dst:dst + 1], coef[:, :, a:a + 1], coef[:, :, b:b + 1], ALU.add
                                ).then_inc(coef_ready, 1)
            dve.wait_ge(coef_ready, 6)
            for t in range(DSUB):
                V.memset(h_f[:, 0, t:t + 1], 0.0).then_inc(st_out[t], 16)

            def tap(acc, src, c, n, add=None):
                return V.scalar_tensor_tensor(out=acc, in0=src, scalar=coef[:, c, n:n + 1],
                                              in1=acc if add is None else add, op0=ALU.mult, op1=ALU.add)

            def edges(band, j):
                return V.tensor_tensor(band[:, 0:LW:LW - 1], band[:, 0:LW:LW - 1],
                                       edge_sb[:, bass.ds(2 * j, 2)], ALU.mult)

            def pair_taps(dst, src, p, g, j, first_done, step, base):
                for k in range(1, 4):
                    for u in range(2):
                        c = 2 * p + u
                        if k == 1:
                            dve.wait_ge(first_done, NC * j + c + 1)
                        else:
                            dve.wait_ge(step, base + 2 * (k - 2) + u + 1)
                        tap(dst[:, c, :], src[:, c, k:k + 2 * LW - 1:2], c, g + k).then_inc(step, 1)
                for u in range(2):
                    dve.wait_ge(step, base + 5 + u)
                    edges(dst[:, 2 * p + u, :], j).then_inc(step, 1)

            def low1(a, batch, p):
                pair_taps(l1, xa, p, H0, a, l1_first, low1_step, (2 * a + p) * N_LOW1)

            def band2(a, batch, c):
                n = (NC * a + c) * N_BAND2
                dve.wait_ge(low1_step, (2 * a + c // 2 + 1) * N_LOW1)
                dve.wait_ge(band2_first, 2 * (NC * a + c + 1))
                for k in range(1, 4):
                    for which, (band, g) in enumerate(((l2, H0), (h2, G0))):
                        if k > 1:
                            dve.wait_ge(band2_step, n + 2 * (k - 1) + which - 1)
                        tap(band[:, c, :], l1[:, c, k:k + 2 * M2 - 1:2], c, g + k).then_inc(band2_step, 1)
                dve.wait_ge(band2_step, n + 5)
                if c == 0 and not first(a):
                    dve.wait_ge(turned, NC * a)
                    dve.wait_ge(st_q, 16 * a)
                V.tensor_scalar(keys[:, c, :], l2[:, c, :], 0.0, None, ALU.min).then_inc(band2_step, 1)

            def keys_sum(a, batch, _):
                dve.wait_ge(exp_done, a + 1)
                for c in range(NC):
                    V.scalar_tensor_tensor(out=keys[:, c, :], in0=l2[:, c, :], scalar=0.0, in1=keys[:, c, :],
                                           op0=ALU.max, op1=ALU.add, accum_out=z_part[:, c:c + 1]
                                           ).then_inc(keys_step, 1)
                dve.wait_ge(keys_step, N_KEYS * a + NC)
                V.tensor_tensor(z_sum[:, :], z_sum[:, :], z_part[:, :], ALU.add).then_inc(keys_step, 1)

            def kv(a, batch, _):
                dve.wait_ge(kv_ready, a + 1)
                V.tensor_tensor(kv_sum[:, :], ps_x[:, :], kv_sum[:, :], ALU.add).then_inc(kv_added, 1)

            def blocks(a, batch, _):
                dve.wait_ge(kv_added, PER_BATCH * (batch + 1))
                V.tensor_tensor(kv_blocks[:, :, :], kv_sum[:, :].rearrange("p (c n) -> p c n", c=NC),
                                mask[:, None, :].to_broadcast([P, NC, P]), ALU.mult).then_inc(blocks_step, 1)
                dve.wait_ge(keys_step, N_KEYS * PER_BATCH * (batch + 1))
                for c in range(NC):
                    V.tensor_scalar(z_heads[:, c, :], head_of[:, c, :], z_sum[:, c:c + 1], None, ALU.mult
                                    ).then_inc(blocks_step, 1)

            def high1(j, batch, p):
                pair_taps(h1, xb, p, G0, j, h1_first, high1_step, (2 * j + p) * N_HIGH1)

            def dens(j, batch, _):
                dve.wait_ge(den_ready, j + 1)
                V.tensor_scalar(den[:, :], ps_y[0:HEADS, 0:QW], ATTN_EPS, None, ALU.add).then_inc(den_step, 1)
                dve.wait_ge(den_step, 2 * j + 1)
                V.reciprocal(den[:, :], den[:, :]).then_inc(den_step, 1)

            def attend(j, batch, c):
                dve.wait_ge(rden_out, NC * j + c + 1)
                V.tensor_tensor(att[:, c % 2, :], ps_x[:, 0:QW], att[:, c % 2, :], ALU.mult).then_inc(att_done, 1)

            def synth2(j, batch, c):
                n = (NC * j + c) * N_SYN2
                u = M2 + 1
                a_, h_ = att[:, c % 2, :], h2_in[:, c, :]
                odd, even = low[:, c % 2, 0:2 * u - 1:2], low[:, c % 2, 1:2 * u:2]
                dve.wait_ge(low_first, 2 * (NC * j + c + 1))
                tap(even, h_[:, 1:1 + u], c, T12).then_inc(syn2_step, 1)
                tap(odd, h_[:, 1:1 + u], c, T23).then_inc(syn2_step, 1)
                dve.wait_ge(syn2_step, n + 1)
                tap(even, h_[:, 2:2 + u], c, T0 + 3).then_inc(syn2_step, 1)
                dve.wait_ge(att_done, NC * j + c + 1)
                dve.wait_ge(syn2_step, n + 2)
                tap(odd, a_[:, 0:u], c, S01).then_inc(syn2_step, 1)
                dve.wait_ge(syn2_step, n + 3)
                tap(even, a_[:, 0:u], c, S0).then_inc(syn2_step, 1)
                dve.wait_ge(syn2_step, n + 4)
                tap(odd, a_[:, 1:1 + u], c, S23).then_inc(syn2_step, 1)
                dve.wait_ge(syn2_step, n + 5)
                tap(even, a_[:, 1:1 + u], c, S12).then_inc(syn2_step, 1)
                dve.wait_ge(syn2_step, n + 7)
                tap(even, a_[:, 2:2 + u], c, S0 + 3).then_inc(syn2_step, 1)
                dve.wait_ge(syn2_step, n + 8)
                edges(low[:, c % 2, :], j).then_inc(syn2_step, 1)

            def synth1a(j, batch, c):
                n = (NC * j + c) * N_SYN1A
                even, odd = s_chan[:, c, 0:TOK - 1:2], s_chan[:, c, 1:TOK:2]
                dve.wait_ge(high1_step, (2 * j + c // 2 + 1) * N_HIGH1)
                if c == 0 and not first(j):
                    dve.wait_ge(s_ready, SUBS * j)
                tap(even, h1[:, c, 0:M1], c, T0, xb[:, c, 3:3 + TOK - 1:2]).then_inc(syn1a_step, 1)
                tap(odd, h1[:, c, 1:1 + M1], c, T01, xb[:, c, 4:4 + TOK - 1:2]).then_inc(syn1a_step, 1)
                dve.wait_ge(syn1a_step, n + 1)
                tap(even, h1[:, c, 1:1 + M1], c, T12).then_inc(syn1a_step, 1)
                dve.wait_ge(syn1a_step, n + 2)
                tap(odd, h1[:, c, 2:2 + M1], c, T23).then_inc(syn1a_step, 1)
                dve.wait_ge(syn1a_step, n + 3)
                tap(even, h1[:, c, 2:2 + M1], c, T0 + 3).then_inc(syn1a_step, 1)

            def synth1b(j, batch, c):
                n = (NC * j + c) * N_SYN1B
                even, odd = s_chan[:, c, 0:TOK - 1:2], s_chan[:, c, 1:TOK:2]
                lw = low[:, c % 2, :]
                dve.wait_ge(syn2_step, (NC * j + c + 1) * N_SYN2)
                dve.wait_ge(syn1a_step, (NC * j + c) * N_SYN1A + 4)
                tap(odd, lw[:, 1:1 + M1], c, S01).then_inc(syn1b_step, 1)
                dve.wait_ge(syn1a_step, (NC * j + c + 1) * N_SYN1A)
                tap(even, lw[:, 0:M1], c, S0).then_inc(syn1b_step, 1)
                dve.wait_ge(syn1b_step, n + 1)
                tap(odd, lw[:, 2:2 + M1], c, S23).then_inc(syn1b_step, 1)
                dve.wait_ge(syn1b_step, n + 2)
                tap(even, lw[:, 1:1 + M1], c, S12).then_inc(syn1b_step, 1)
                dve.wait_ge(syn1b_step, n + 4)
                tap(even, lw[:, 2:2 + M1], c, S0 + 3).then_inc(syn1b_step, 1)

            def norm2(j, batch, t):
                s = SUBS * j + t
                dve.wait_ge(s_squares, s + 1)
                V.scalar_tensor_tensor(out=x1[:, t, :], in0=x1[:, t, :], scalar=rs1[:, t, 1:2],
                                       in1=gamma_b[:, :], op0=ALU.add, op1=ALU.mult).then_inc(s_centred, 1)
                dve.wait_ge(s_centred, s + 1)
                dve.wait_ge(x_beta, s + 1)
                dve.wait_ge(rstd1, s + 1)
                V.scalar_tensor_tensor(out=x1[:, t, :], in0=x1[:, t, :], scalar=rs1[:, t, 4:5],
                                       in1=xt[:, t % 4, :], op0=ALU.mult, op1=ALU.add,
                                       accum_out=rs2[:, t, 0:1]).then_inc(r_ready, 1)

            def norm3(j, batch, t):
                dve.wait_ge(x1_hi_ready, SUBS * j + t + 1)
                cols = slice((t % DSUB) * P, (t % DSUB + 1) * P)
                V.tensor_tensor(x1_lo[:, t // DSUB, :, cols], ps_y[:, :].rearrange("p (c n) -> p c n", c=NC),
                                x1_hi[:, t // DSUB, :, cols], ALU.subtract).then_inc(x1_lo_ready, 1)

            steps = {"low1": low1, "band2": band2, "keys": keys_sum, "kv": kv, "blocks": blocks, "high1": high1,
                     "dens": dens, "attend": attend, "synth2": synth2, "synth1a": synth1a, "synth1b": synth1b,
                     "norm2": norm2, "norm3": norm3}

            def out1(a, batch, c):
                dve.wait_ge(l1_first, NC * a + c + 1)
                edges(l1[:, c, :], a).then_inc(low1_step, N_LOW1 // 2)

            def out2(a, batch, c):
                dve.wait_ge(band2_first, 2 * (NC * a + c + 1))
                V.tensor_scalar(keys[:, c, :], l2[:, c, :], 0.0, None, ALU.min).then_inc(band2_step, N_BAND2)

            def kv_add(a, batch, _):
                kv(a, batch, 0)
                if isinstance(a, int) and a == PER_BATCH - 1:
                    blocks(a, batch, 0)
                    dve.wait_ge(blocks_step, N_BLOCKS)
                    V.memset(kv_sum[:], 0.0).then_inc(sums_zero, 1)
                    V.memset(z_sum[:], 0.0).then_inc(sums_zero, 1)
                    dve.wait_ge(sums_zero, 2)

            def first_high(a, batch, _):
                if isinstance(a, int) and a == PER_BATCH:
                    high1(0, 0, 0)

            def h_out(j, batch, c):
                dve.wait_ge(h1_first, c + 1)
                edges(h1[:, c, :], j).then_inc(high1_step, N_HIGH1 // 2)

            before_analyses(dve, {**{name: steps[name] for name in steps if name != "kv"}, "out1": out1,
                                  "out2": out2, "kv_add": kv_add, "mix": first_high})
            run = before({**steps, "h_out": h_out})
            run(FIRST_MIX + FIRST_NORM, 0, 0)

            def body(i, batch, analysis, last):
                for b in range(2):
                    B = 2 * i + b
                    for k in range(NH):
                        n = NH * B + k
                        if k == 0:
                            beside(b, k, i, batch, analysis, last, steps)
                        dve.wait_ge(silu_done, n + 1)
                        V.scalar_tensor_tensor(out=h_f[:, k % 2, :], in0=ps_gu[k % 2][1][:, :],
                                               scalar=WSCALE * H_SCALE / X1_SCALE, in1=gate_s[:, k % 2, :],
                                               op0=ALU.mult, op1=ALU.mult).then_inc(h_mul, 1)
                        if 0 < k < NH - 1:
                            beside(b, k, i, batch, analysis, last, steps)
                        dve.wait_ge(hi_done, n + 1)
                        V.tensor_tensor(h_lo[:, k, :], h_f[:, k % 2, :], h_hi[:, k, :], ALU.subtract
                                        ).then_inc(lo_done, 1)
                        if k == NH - 1:
                            beside(b, k, i, batch, analysis, last, steps)
                    for t in range(DSUB):
                        n = DSUB * B + t
                        beside(b, NH + t, i, batch, analysis, last, steps)
                        beside(b, NH + t + 0.5, i, batch, analysis, last, steps)
                        dve.wait_ge(d_ready, n + 1)
                        dve.wait_ge(st_out[t], 16 * (B + 1))
                        V.scalar_tensor_tensor(out=z[:, t, :], in0=ps_d[t % 2][:, :],
                                               scalar=WSCALE * X1_SCALE / H_SCALE, in1=x1[:, b * DSUB + t, :],
                                               op0=ALU.mult, op1=ALU.add, accum_out=rs3[:, t, 0:1]
                                               ).then_inc(z_done, 1)

            iterations(dve, body)


def kernel(L0_attn_x, L0_attn_h_filter, L0_attn_g_filter, L0_attn_h_synth, L0_attn_g_synth,
           L0_attn_norm_gamma, L0_attn_norm_beta, L0_ffn_w_gate, L0_ffn_w_up, L0_ffn_w_down):
    import numpy as np
    import concourse.bacc as bacc
    from concourse.bass_utils import run_bass_kernel_spmd

    x = np.ascontiguousarray(L0_attn_x)
    padded = np.zeros((P, BATCHES, NC, SEQ + 6), x.dtype)
    padded[:, :, :, 3:3 + SEQ] = x.reshape(BATCHES, SEQ, NC, P).transpose(3, 0, 2, 1)
    x_chan = np.stack([padded[:, j // PER_BATCH, :, j % PER_BATCH * TOK:j % PER_BATCH * TOK + XW]
                       for j in range(ITERS)], axis=1)
    taps = np.stack([np.asarray(f).reshape(4, NC, P) for f in
                     (L0_attn_h_filter, L0_attn_g_filter, L0_attn_h_synth, L0_attn_g_synth)])
    taps = np.ascontiguousarray(taps.transpose(3, 2, 0, 1).reshape(P, NC, 16))
    gamma = np.ascontiguousarray(np.broadcast_to(np.asarray(L0_attn_norm_gamma), (P, C)))
    beta = np.ascontiguousarray(np.broadcast_to(np.asarray(L0_attn_norm_beta), (P, C)))
    wg = np.asarray(L0_ffn_w_gate).reshape(HID, NC, P).transpose(2, 1, 0).reshape(P, NC * HID)
    wu = np.asarray(L0_ffn_w_up).reshape(HID, NC, P).transpose(2, 1, 0).reshape(P, NC * HID)
    wd = np.asarray(L0_ffn_w_down).reshape(C, NH, P).transpose(2, 1, 0).reshape(P, NH * C)
    weights = np.ascontiguousarray(np.concatenate([wg, wu, wd], axis=1))
    edge = np.ones((P, ITERS, 2), np.float32)
    edge[:, 0::PER_BATCH, 0] = 0.0
    edge[:, PER_BATCH - 1::PER_BATCH, 1] = 0.0
    edge = edge.reshape(P, 2 * ITERS)
    identity = np.eye(P, dtype=np.float32)
    block_mask = np.kron(np.eye(P // HEAD, dtype=np.float32), np.ones((HEAD, HEAD), np.float32))
    head_of = (np.arange(C) // HEAD)[:, None] == np.arange(HEADS)[None, :]
    head_mask = np.ascontiguousarray(head_of.reshape(NC, P, HEADS).transpose(1, 0, 2).astype(np.float32))
    head_spread = np.ascontiguousarray(head_of.reshape(NC, P, HEADS).transpose(2, 0, 1).astype(np.float32))

    nc = bacc.Bacc("TRN2", target_bir_lowering=False, num_devices=1, dynamic_dma_scratch_size=1024)
    arrays, args = {}, []
    for name, a in (("x_tok", x.reshape(BATCHES * SEQ, C)), ("x_chan", x_chan), ("taps", taps), ("gamma", gamma), ("beta", beta),
                    ("edge", edge), ("weights", weights), ("identity", identity), ("block_mask", block_mask),
                    ("head_mask", head_mask), ("head_spread", head_spread)):
        arrays[name] = a
        args.append(nc.dram_tensor(name, a.shape, mybir.dt.from_np(a.dtype), kind="ExternalInput").ap())
    out = nc.dram_tensor("out", (BATCHES * SEQ, C), F32, kind="ExternalOutput").ap()
    mixer_ffn(nc, *args, out)
    result = run_bass_kernel_spmd(nc, [arrays], core_ids=[0])
    return result.results[0]["out"].reshape(BATCHES, SEQ, C)
```
